# Optimizing a Trainium2 kernel written in Bass

```python
import numpy as np
import jax
import jax.numpy as jnp

def _softmax(x, axis=-1):
    return jax.nn.softmax(x, axis=axis)

def _gelu(x):
    return jax.nn.gelu(x, approximate=True)

def _silu(x):
    return jax.nn.silu(x)

def _sigmoid(x):
    return jax.nn.sigmoid(x)

def _layernorm(x, axis=-1, eps=1e-05):
    m = jnp.mean(x, axis=axis, keepdims=True)
    v = jnp.var(x, axis=axis, keepdims=True)
    return (x - m) / jnp.sqrt(v + eps)

def _scatter_add(tgt, idx, src, axis=0):
    return tgt.at[idx].add(src)

def _segment_sum(src, seg, n):
    return jax.ops.segment_sum(src, seg, n)
kernel_name = 'mk_adaln_ffn_d2_seqx_r8_34627f'

def setup_inputs(seed: int=0):
    np.random.seed(seed)
    _w = jnp.asarray

    def _rec_inputs():
        import jax
        import jax.numpy as jnp
        _rk = jax.random.key(seed)
        x = -7.109e-05 + 0.9999 * jax.random.normal(jax.random.fold_in(_rk, 1), (8, 128, 512), jnp.float32)
        _lenS = 128 - jax.random.randint(jax.random.fold_in(_rk, 7), (8,), 0, max(1, 128 // 4) + 1, jnp.int32)
        _lenS2 = 128 - jax.random.randint(jax.random.fold_in(_rk, 8), (8,), 0, max(1, 128 // 4) + 1, jnp.int32)
        itok_B_1_14 = jax.random.randint(jax.random.fold_in(_rk, 11), (8,), 1, 15, jnp.int32)
        itok_Bx16_0_63 = jax.random.randint(jax.random.fold_in(_rk, 12), (8, 16), 0, 64, jnp.int32)
        itok_B_207_1644 = jax.random.randint(jax.random.fold_in(_rk, 13), (8,), 207, 1645, jnp.int32)
        return (x, itok_B_1_14, itok_Bx16_0_63, itok_B_207_1644)
    x, itok_B_1_14, itok_Bx16_0_63, itok_B_207_1644 = _rec_inputs()

    def _L0_cond_setup():
        import jax, jax.numpy as jnp
        import numpy as np
        B, S, D_IN = (8, 256, 512)
        A, D_OUT = (16, 512)
        key = jax.random.key(seed)
        k1, k2, k3 = jax.random.split(key, 3)
        x = jax.random.normal(k1, (B, S, D_IN), dtype=jnp.float32)
        weight = jax.random.normal(k2, (A, D_OUT, D_IN), dtype=jnp.float32) * 0.02
        adapter_ids = jax.random.randint(k3, (B,), 0, A, dtype=jnp.int64)
        return {'x': x, 'weight': weight, 'adapter_ids': adapter_ids}
    _L0_cond_all = _L0_cond_setup()
    _L0_cond_in = {k: v for k, v in _L0_cond_all.items() if k in ('weight',)}
    del _L0_cond_all

    def _L0_ffn_setup():
        import jax, jax.numpy as jnp
        import numpy as np
        SCALING = 16.0 / 8.0
        GAMMA = 1.0
        EPS = 1e-12
        key = jax.random.key(seed)
        ks = jax.random.split(key, 8)
        B, T, H, O = (4, 256, 512, 512)
        E_tot, E_act, r = (16, 4, 8)
        return {'x': jax.random.normal(ks[0], (B, T, H), jnp.float32), 'W_base': jax.random.normal(ks[1], (O, H), jnp.float32) * 0.02, 'b_base': jax.random.normal(ks[2], (O,), jnp.float32) * 0.02, 'lora_A': jax.random.normal(ks[3], (E_tot, r, H), jnp.float32) * 0.02, 'lora_B': jax.random.normal(ks[4], (E_tot, O, r), jnp.float32) * 0.02, 'router_W': jax.random.normal(ks[5], (E_tot, H), jnp.float32) * 0.02, 'router_b': jax.random.normal(ks[6], (E_tot,), jnp.float32) * 0.02, 'domain_prior': jax.random.uniform(ks[7], (E_tot,), jnp.float32), 'active': jnp.arange(E_act, dtype=jnp.int32)}
    _L0_ffn_all = _L0_ffn_setup()
    _L0_ffn_in = {k: v for k, v in _L0_ffn_all.items() if k in ('W_base', 'b_base', 'lora_A', 'lora_B', 'router_W', 'router_b', 'domain_prior', 'active')}
    del _L0_ffn_all

    def _L1_cond_setup():
        import jax, jax.numpy as jnp
        import numpy as np
        B, S, HID = (4, 128, 512)
        D, HQ, HK = (128, 32, 8)
        PAGES, PSIZE, NPP = (64, 32, 16)
        THETA = 10000.0
        EPS = 1e-06
        SCALE = 1.0 / float(np.sqrt(D))

        def _rmsnorm(t, w):
            var = jnp.mean(t * t, axis=-1, keepdims=True)
            return t * jax.lax.rsqrt(var + EPS) * w

        def _rope(t, pos):
            inv_freq = 1.0 / THETA ** (jnp.arange(0, D, 2, dtype=jnp.float32) / D)
            freqs = pos[..., None].astype(jnp.float32) * inv_freq
            cos = jnp.cos(freqs)[:, :, None, :]
            sin = jnp.sin(freqs)[:, :, None, :]
            t1, t2 = (t[..., :D // 2], t[..., D // 2:])
            return jnp.concatenate([t1 * cos - t2 * sin, t2 * cos + t1 * sin], axis=-1)
        key = jax.random.key(seed)
        ks = jax.random.split(key, 10)
        x = jax.random.normal(ks[0], (B, S, HID), jnp.float32)
        Wq = jax.random.normal(ks[1], (HQ * D, HID), jnp.float32) * 0.02
        Wk = jax.random.normal(ks[2], (HK * D, HID), jnp.float32) * 0.02
        Wv = jax.random.normal(ks[3], (HK * D, HID), jnp.float32) * 0.02
        Wo = jax.random.normal(ks[4], (HID, HQ * D), jnp.float32) * 0.02
        q_norm_w = jax.random.uniform(ks[5], (D,), jnp.float32)
        k_norm_w = jax.random.uniform(ks[6], (D,), jnp.float32)
        k_cache = jax.random.normal(ks[7], (PAGES, PSIZE, HK, D), jnp.float32)
        v_cache = jax.random.normal(ks[8], (PAGES, PSIZE, HK, D), jnp.float32)
        block_table = jnp.arange(B * NPP, dtype=jnp.int32).reshape(B, NPP)
        cache_seqlens = jax.random.randint(ks[9], (B,), 0, 475).astype(jnp.int32)
        return dict(x=x, Wq=Wq, Wk=Wk, Wv=Wv, Wo=Wo, q_norm_w=q_norm_w, k_norm_w=k_norm_w, k_cache=k_cache, v_cache=v_cache, block_table=block_table, cache_seqlens=cache_seqlens)
    _L1_cond_all = _L1_cond_setup()
    _L1_cond_in = {k: v for k, v in _L1_cond_all.items() if k in ('Wq', 'Wk', 'Wv', 'Wo', 'q_norm_w', 'k_norm_w', 'k_cache', 'v_cache')}
    del _L1_cond_all

    def _L1_ffn_setup():
        import jax, jax.numpy as jnp
        import numpy as np
        FP8_MAX = 448.0

        def fwht(x):
            d = x.shape[-1]
            shape = x.shape
            y = x.reshape(-1, d)
            h = 2
            while h <= d:
                y = y.reshape(-1, h)
                half = h // 2
                a, b = (y[:, :half], y[:, half:])
                y = jnp.concatenate([a + b, a - b], axis=-1).reshape(-1, d)
                h *= 2
            return (y * d ** (-0.5)).reshape(shape)
        key = jax.random.key(seed)
        k1, k2, k3 = jax.random.split(key, 3)
        B, S, D_IN, D_OUT = (4, 256, 512, 512)
        x = jax.random.normal(k1, (B, S, D_IN), dtype=jnp.float32)
        w = jax.random.normal(k2, (D_OUT, D_IN), dtype=jnp.float32) * 0.02
        wh = fwht(w)
        scales = jnp.max(jnp.abs(wh), axis=1) / FP8_MAX
        weight_q = (wh / scales[:, None]).astype(jnp.float8_e4m3fn).astype(jnp.float32)
        bias = jax.random.normal(k3, (D_OUT,), dtype=jnp.float32)
        return {'x': x, 'weight_q': weight_q, 'scales': scales, 'bias': bias}
    _L1_ffn_all = _L1_ffn_setup()
    _L1_ffn_in = {k: v for k, v in _L1_ffn_all.items() if k in ('weight_q', 'scales', 'bias')}
    del _L1_ffn_all
    return {'x': x, 'itok_B_1_14': itok_B_1_14, 'itok_Bx16_0_63': itok_Bx16_0_63, 'itok_B_207_1644': itok_B_207_1644, 'L0_cond_weight': _L0_cond_in['weight'], 'L0_ffn_W_base': _L0_ffn_in['W_base'], 'L0_ffn_b_base': _L0_ffn_in['b_base'], 'L0_ffn_lora_A': _L0_ffn_in['lora_A'], 'L0_ffn_lora_B': _L0_ffn_in['lora_B'], 'L0_ffn_router_W': _L0_ffn_in['router_W'], 'L0_ffn_router_b': _L0_ffn_in['router_b'], 'L0_ffn_domain_prior': _L0_ffn_in['domain_prior'], 'L0_ffn_active': _L0_ffn_in['active'], 'L1_cond_Wq': _L1_cond_in['Wq'], 'L1_cond_Wk': _L1_cond_in['Wk'], 'L1_cond_Wv': _L1_cond_in['Wv'], 'L1_cond_Wo': _L1_cond_in['Wo'], 'L1_cond_q_norm_w': _L1_cond_in['q_norm_w'], 'L1_cond_k_norm_w': _L1_cond_in['k_norm_w'], 'L1_cond_k_cache': _L1_cond_in['k_cache'], 'L1_cond_v_cache': _L1_cond_in['v_cache'], 'L1_ffn_weight_q': _L1_ffn_in['weight_q'], 'L1_ffn_scales': _L1_ffn_in['scales'], 'L1_ffn_bias': _L1_ffn_in['bias']}

def reference(x, itok_B_1_14, itok_Bx16_0_63, itok_B_207_1644, L0_cond_weight, L0_ffn_W_base, L0_ffn_b_base, L0_ffn_lora_A, L0_ffn_lora_B, L0_ffn_router_W, L0_ffn_router_b, L0_ffn_domain_prior, L0_ffn_active, L1_cond_Wq, L1_cond_Wk, L1_cond_Wv, L1_cond_Wo, L1_cond_q_norm_w, L1_cond_k_norm_w, L1_cond_k_cache, L1_cond_v_cache, L1_ffn_weight_q, L1_ffn_scales, L1_ffn_bias):
    import jax
    import jax.numpy as jnp

    def _L0_cond_ref(x, weight, adapter_ids):
        import jax, jax.numpy as jnp
        import numpy as np
        B, S, D_IN = (8, 256, 512)
        A, D_OUT = (16, 512)
        w = weight[adapter_ids]
        return jnp.einsum('bij,bkj->bik', x, w)

    def _L0_ffn_ref(x, W_base, b_base, lora_A, lora_B, router_W, router_b, domain_prior, active):
        import jax, jax.numpy as jnp
        import numpy as np
        SCALING = 16.0 / 8.0
        GAMMA = 1.0
        EPS = 1e-12
        y = jnp.einsum('bth,oh->bto', x, W_base) + b_base
        A = lora_A[active]
        Bm = lora_B[active]
        z = jnp.einsum('bth,erh->bter', x, A)
        contribs = jnp.einsum('bter,eor->bteo', z, Bm) * SCALING
        logits = jnp.einsum('bth,eh->bte', x, router_W) + router_b
        logits = logits[..., active]
        prior = domain_prior[active]
        alpha = jax.nn.softmax(jnp.log(prior + EPS) + logits / GAMMA, axis=-1)
        return y + jnp.einsum('bteo,bte->bto', contribs, alpha)

    def _L1_cond_ref(x, Wq, Wk, Wv, Wo, q_norm_w, k_norm_w, k_cache, v_cache, block_table, cache_seqlens):
        import jax, jax.numpy as jnp
        import numpy as np
        B, S, HID = (4, 128, 512)
        D, HQ, HK = (128, 32, 8)
        PAGES, PSIZE, NPP = (64, 32, 16)
        THETA = 10000.0
        EPS = 1e-06
        SCALE = 1.0 / float(np.sqrt(D))

        def _rmsnorm(t, w):
            var = jnp.mean(t * t, axis=-1, keepdims=True)
            return t * jax.lax.rsqrt(var + EPS) * w

        def _rope(t, pos):
            inv_freq = 1.0 / THETA ** (jnp.arange(0, D, 2, dtype=jnp.float32) / D)
            freqs = pos[..., None].astype(jnp.float32) * inv_freq
            cos = jnp.cos(freqs)[:, :, None, :]
            sin = jnp.sin(freqs)[:, :, None, :]
            t1, t2 = (t[..., :D // 2], t[..., D // 2:])
            return jnp.concatenate([t1 * cos - t2 * sin, t2 * cos + t1 * sin], axis=-1)
        bsz, seqlen, _ = x.shape
        q = jnp.einsum('bsd,ed->bse', x, Wq).reshape(bsz, seqlen, HQ, D)
        k = jnp.einsum('bsd,ed->bse', x, Wk).reshape(bsz, seqlen, HK, D)
        v = jnp.einsum('bsd,ed->bse', x, Wv).reshape(bsz, seqlen, HK, D)
        q = _rmsnorm(q, q_norm_w)
        k = _rmsnorm(k, k_norm_w)
        pos = cache_seqlens[:, None] + jnp.arange(seqlen)[None, :]
        q = _rope(q, pos)
        k = _rope(k, pos)
        L = NPP * PSIZE
        kc = k_cache[block_table].reshape(bsz, L, HK, D)
        vc = v_cache[block_table].reshape(bsz, L, HK, D)
        k_all = jnp.concatenate([kc, k], axis=1)
        v_all = jnp.concatenate([vc, v], axis=1)
        valid_c = jnp.arange(L)[None, :] < cache_seqlens[:, None]
        valid = jnp.concatenate([valid_c, jnp.ones((bsz, seqlen), dtype=bool)], axis=1)
        rep = HQ // HK
        k_all = jnp.repeat(k_all, rep, axis=2)
        v_all = jnp.repeat(v_all, rep, axis=2)
        scores = jnp.einsum('bqhd,bkhd->bhqk', q, k_all) * SCALE
        scores = jnp.where(valid[:, None, None, :], scores, -1e+30)
        probs = jax.nn.softmax(scores, axis=-1)
        o = jnp.einsum('bhqk,bkhd->bqhd', probs, v_all)
        o = o.reshape(bsz, seqlen, HQ * D)
        return jnp.einsum('bse,de->bsd', o, Wo)

    def _L1_ffn_ref(x, weight_q, scales, bias):
        import jax, jax.numpy as jnp
        import numpy as np
        FP8_MAX = 448.0

        def fwht(x):
            d = x.shape[-1]
            shape = x.shape
            y = x.reshape(-1, d)
            h = 2
            while h <= d:
                y = y.reshape(-1, h)
                half = h // 2
                a, b = (y[:, :half], y[:, half:])
                y = jnp.concatenate([a + b, a - b], axis=-1).reshape(-1, d)
                h *= 2
            return (y * d ** (-0.5)).reshape(shape)
        xh = fwht(x)
        sx = jnp.max(jnp.abs(xh), axis=-1, keepdims=True) / FP8_MAX
        xq = xh / sx
        xq = xq.astype(jnp.float8_e4m3fn).astype(jnp.float32)
        acc = jnp.einsum('bsd,od->bso', xq, weight_q)
        return acc * sx * scales + bias
    x = x + _L0_ffn_ref(_L0_cond_ref(x, L0_cond_weight, itok_B_1_14), L0_ffn_W_base, L0_ffn_b_base, L0_ffn_lora_A, L0_ffn_lora_B, L0_ffn_router_W, L0_ffn_router_b, L0_ffn_domain_prior, L0_ffn_active)
    x = x + _L1_ffn_ref(_L1_cond_ref(x, L1_cond_Wq, L1_cond_Wk, L1_cond_Wv, L1_cond_Wo, L1_cond_q_norm_w, L1_cond_k_norm_w, L1_cond_k_cache, L1_cond_v_cache, itok_Bx16_0_63, itok_B_207_1644), L1_ffn_weight_q, L1_ffn_scales, L1_ffn_bias)
    return x

_drawn_inputs = setup_inputs


def setup_inputs(seed=0):
    import zlib

    import numpy as np

    out = dict(_drawn_inputs(seed))
    spreads = {}
    factors = {'L0_ffn_b_base': 4.15,
     'L0_ffn_lora_A': 5.645,
     'L0_ffn_lora_B': 5.677,
     'L0_ffn_router_W': 8.0,
     'L0_ffn_router_b': 8.0,
     'L0_ffn_domain_prior': 8.0,
     'L1_cond_Wq': 5.372,
     'L1_cond_Wk': 8.0,
     'L1_cond_Wv': 8.0,
     'L1_cond_Wo': 2.9,
     'L1_cond_q_norm_w': 8.0,
     'L1_cond_k_norm_w': 8.0,
     'L1_cond_k_cache': 5.393,
     'L1_cond_v_cache': 2.971,
     'L1_ffn_weight_q': 2.861,
     'L1_ffn_scales': 8.0,
     'L1_ffn_bias': 6.353}
    for name, (base, spread) in spreads.items():
        noise = np.random.default_rng([zlib.crc32(name.encode()), seed]).standard_normal(out[name].shape)
        drawn = base * np.exp(spread * noise) if base else spread * noise
        out[name] = jnp.asarray(drawn.astype(out[name].dtype))
    for name, factor in factors.items():
        out[name] = (out[name] * factor).astype(out[name].dtype)
    return out
```

```python
import concourse.bass as bass
from concourse import mybir
from contextlib import ExitStack

F32 = mybir.dt.float32
F32R = mybir.dt.float32r
I32 = mybir.dt.int32
U32 = mybir.dt.uint32
ALU = mybir.AluOpType
ACT = mybir.ActivationFunctionType
AX = mybir.AxisListType.X

B, S, DM = 8, 128, 512
CH = DM // 128
D, HQ, HK = 128, 32, 8
G = HQ // HK
ADAPTERS = 16
PAGES, PSIZE, NPP = 64, 32, 16
L = NPP * PSIZE
CT = L // 128
KT = CT + 1
KEYS = L + S
PPT = 128 // PSIZE
NE, RK = 16, 8
NACT = 4
ZCOLS = NE * RK
L0COLS = DM + ZCOLS + NE
STEPS = HK * B
WP = G * D + 2 * D
WCOLS = CH * WP + G * DM
WC = WCOLS // B
AHEAD = B + 1
SCALE = D ** -0.5
NORM_EPS = 1e-6
PRIOR_EPS = 1e-12
LORA_SCALE = 2.0
FP8_MAX = 448.0
MASKED = -1e30
LOWEST = -3e38
PI = 3.141592653589793
PI_IN = 3.1415925
TWO_PI_PARTS = (6.28125, 0.0019350051879882812, 2 * PI - 6.28125 - 0.0019350051879882812)
ROUND_INT = 1.5 * 2.0 ** 23
EXP_BITS = 0x7F800000
MIN_E4M3 = 2.0 ** -6
ROUND_E4M3 = 1.5 * 2.0 ** 20


class Step:

    def __init__(self, eng, value, par, spare=None):
        self.eng, self.value, self.par, self.spare = eng, value, par % 2, spare
        self.fixed = isinstance(value, int)

    def parity(self, d=0):
        return (self.par + d) % 2

    def number(self, f):
        return f(self.value) if self.fixed else self.eng.snap(f(self.value))

    def has(self, d, n):
        return not self.fixed or 0 <= self.value + d < n

    def wait(self, sem, d=0):
        if self.fixed:
            if self.value + d >= 0:
                self.eng.wait_ge(sem, self.value + d + 2)
        else:
            self.eng.wait_ge(sem, self.eng.snap(self.value + (d + 2)))

    def hold(self):
        self.eng.sem_inc(self.spare, 1)

    def wait_dma(self, sems, d=0, dmas=1):
        p = self.parity(d)
        if self.fixed:
            self.eng.wait_ge(sems[p], 16 * dmas * ((self.value + d) // 2 + 1))
        else:
            self.eng.wait_ge(sems[p], self.eng.snap((self.value + (d - p + 2)) * (8 * dmas)))


def run_steps(eng, first, loop_first, loop_end, end, body, spare=None):
    for i in range(first, loop_first):
        body(Step(eng, i, i, spare))
    with eng.Fori(loop_first // 2, loop_end // 2) as pair:
        for u in range(2):
            body(Step(eng, eng.snap(pair * 2 + u), u, spare))
    for i in range(loop_end, end):
        body(Step(eng, i, i, spare))


def events(ctx, nc, eng_names):
    sems, by_engine = {}, {}
    for engine, names in eng_names.items():
        by_engine[engine] = []
        for name in names.split():
            sems[name] = ctx.enter_context(nc.semaphore(name))
            by_engine[engine].append(sems[name])
    return sems, by_engine


def flat(ap):
    return ap.rearrange("o p n -> (o p) n")


def split3(nc, out, parts, first, last):
    n = len(parts)
    for j, ((a_hi, a_lo), (b_hi, b_lo)) in enumerate(parts):
        nc.tensor.matmul(out, a_hi, b_hi, start=first and j == 0, stop=False)
        nc.tensor.matmul(out, a_hi, b_lo, start=False, stop=False)
        done = nc.tensor.matmul(out, a_lo, b_hi, start=False, stop=last and j == n - 1)
    return done


def first_layer(nc, sem_ctx, s_spare, t, ident, w_hi, w_lo, attn, scratch):
    x1t_dram, x1_dram, rope_dram, mask_dram = scratch
    ctx = ExitStack()
    with ctx:
        def sb(name, shape, dt=F32):
            return ctx.enter_context(nc.sbuf_tensor(name, shape, dt))

        def bank(name):
            return ctx.enter_context(nc.psum_tensor(name, [128, 512], F32))

        def sem(name):
            return sem_ctx.enter_context(nc.semaphore(name))

        xt = [sb(f"xt{p}", [128, CH * S]) for p in range(2)]
        xn = [sb(f"xn{p}", [128, DM]) for p in range(2)]
        wc = [sb(f"wc{p}", [128, CH * DM]) for p in range(2)]
        raw = [sb(f"raw_a{p}", [128, WC]) for p in range(2)]
        w0 = sb("w0", [128, CH, L0COLS])
        lora_b = sb("lora_b", [128, DM])
        bias = sb("bias0", [128, DM])
        router_b = sb("router_b", [128, NE])
        prior = sb("prior", [128, NE])
        active = sb("active", [128, NACT], I32)
        seq_i = sb("seq_i", [128, B], I32)
        invf = sb("invf", [128, D // 2])
        norm_w = sb("norm_w", [128, 2 * D])
        c_sb = [sb(f"c_sb{p}", [128, DM]) for p in range(2)]
        ct = [sb(f"ct{p}", [128, CH * S]) for p in range(2)]
        xb = [sb(f"xb{p}", [128, DM]) for p in range(2)]
        x1 = [sb(f"x1{p}", [128, DM]) for p in range(2)]
        x1t = [sb(f"x1t{p}", [128, 2 * CH * S], F32R) for p in range(2)]
        logit = sb("logit", [128, NE])
        top = sb("top", [128, 1])
        ntop = sb("ntop", [128, 1])
        expl = sb("expl", [128, NE])
        alpha = sb("alpha", [128, NE])
        total = sb("total", [128, 1])
        rtotal = sb("rtotal", [128, 1])
        zs = sb("zs", [128, ZCOLS])
        zst = sb("zst", [128, S])
        act_f = sb("act_f", [128, NACT])
        expert = sb("expert", [128, NE])
        times = sb("times", [128, NE])
        hit = sb("hit", [128, NE])
        unused = sb("unused", [128, NE])
        lprior = sb("lprior", [128, NE])
        lbias = sb("lbias", [128, NE])
        eps_col = sb("eps_col", [128, 1])
        seq_f = sb("seq_f", [128, B])
        tok = sb("tok", [128, 1])
        pos = sb("pos", [128, B])
        key_no = sb("key_no", [128, L])
        angle = sb("angle", [128, B, D // 2])
        turns = sb("turns", [128, B, D // 2])
        cos = sb("cos", [128, B, D // 2])
        sin = sb("sin", [128, B, D // 2])
        rope = attn[:, :].rearrange("p (b n) -> p b n", b=B)
        mask = sb("mask_all", [128, B, KEYS])

        c_bank = bank("c_bank")
        ct_bank = bank("ct_bank")
        z_bank = [bank(f"z_bank{p}") for p in range(2)]
        y_bank = [bank(f"y_bank{p}") for p in range(2)]
        zt_bank = bank("zt_bank")
        xt_bank = bank("xt_bank")

        ev, mine = events(sem_ctx, nc, {
            "pe": "c_done ct_put z_put y_put zt_put x1_done x1t_put",
            "act": "c_out ct_out expl_out zst_out x1t_hi w_hi_a",
            "dve": "logit_out zs_out x1_out x1t_lo",
            "pool": "xb_out w_lo_a",
        })
        s_xt = [sem(f"s_xt{p}") for p in range(2)]
        s_xn = [sem(f"s_xn{p}") for p in range(2)]
        s_wc = [sem(f"s_wc{p}") for p in range(2)]
        s_raw = [sem(f"s_raw_a{p}") for p in range(2)]
        s_st = [sem(f"s_st{p}") for p in range(2)]
        s_w0, s_rows, s_tab, s_consts = sem("s_w0"), sem("s_rows"), sem("s_tab"), sem("s_consts")
        s_v, s_prior, s_sin = sem("s_v"), sem("s_prior"), sem("s_sin")
        s_tables, s_router = sem("s_tables"), sem("s_router")

        block = ctx.enter_context(nc.Block())
        END = B + 2

        @block.sync
        def _(sp):
            rows = [(router_b, t["router_b"]), (prior, t["prior"]), (active, t["active"]),
                    (seq_i, t["seqlens"]), (invf, t["inv_freq"]), (norm_w, t["norm_w"]),
                    (bias, t["b_base"])]

            def body(st):
                p = st.parity()
                if st.has(0, B):
                    i = st.value
                    adapter = sp.value_load(t["adapters"][0:1, bass.ds(i, 1)], min_val=0, max_val=ADAPTERS - 1)
                    st.wait(ev["c_done"], -2)
                    st.hold()
                    sp.dma_start(xt[p][:, :], flat(t["xt"][bass.ds(i, 1)])).then_inc(s_xt[p], 16)
                    sp.dma_start(wc[p][:, :], flat(t["adapter_w"][bass.ds(adapter, 1)])).then_inc(s_wc[p], 16)
                    st.wait(ev["xb_out"], -2)
                    st.hold()
                    sp.dma_start(xn[p][:, :], flat(t["x"][bass.ds(i, 1)])).then_inc(s_xn[p], 16)
                if st.has(0, AHEAD):
                    st.wait(ev["w_lo_a"], -2)
                    st.hold()
                    sp.dma_start(raw[p][:, :], flat(t["weights"][bass.ds(st.value, 1)])).then_inc(s_raw[p], 16)
                if st.has(-2, B):
                    st.wait(ev["x1t_lo"], -2)
                    st.wait(ev["x1t_hi"], -2)
                    st.hold()
                    sp.dma_start(flat(x1_dram[bass.ds(st.number(lambda v: v - 2), 1)]), x1[p][:, :]).then_inc(s_st[p], 16)
                    sp.dma_start(flat(x1t_dram[bass.ds(st.number(lambda v: v - 2), 1)]), x1t[p][:, :].bitcast(F32)).then_inc(s_st[p], 16)
                if st.fixed and st.value == 0:
                    for c in range(CH):
                        sp.dma_start(w0[:, c, :], t["w0"][:, c, :]).then_inc(s_w0, 16)
                    sp.dma_start(lora_b[:, :], t["lora_b"]).then_inc(s_w0, 16)
                    for row, src in rows:
                        sp.dma_start(row[:, :], src.partition_broadcast(128)).then_inc(s_rows, 16)

            run_steps(sp, 0, 2, B, END, body, s_spare)
            sp.wait_ge(s_tables, 2)
            sp.dma_start(rope_dram.rearrange("b p n -> p b n"), rope).then_inc(s_tab, 16)
            sp.dma_start(mask_dram.rearrange("b p n -> p b n"), mask[:, :, :]).then_inc(s_tab, 16)
            sp.wait_ge(s_tab, 32)
            for p in range(2):
                sp.wait_ge(s_st[p], 16 * B)

        @block.tensor
        def _(pe):
            for s in mine["pe"]:
                pe.sem_inc(s, 1)
            pe.wait_ge(s_consts, 2)

            def body(st):
                p, q = st.parity(), st.parity(-1)
                if st.has(-2, B):
                    st.wait(ev["zs_out"], -2)
                    st.wait(ev["zst_out"], -3)
                    nc.tensor.transpose(zt_bank[:, 0:S], zs[:, :], ident[:, :]).then_inc(ev["zt_put"], 1)
                if st.has(0, B):
                    st.wait_dma(s_xt, 0)
                    st.wait_dma(s_wc, 0)
                    st.wait(ev["c_out"], -1)
                    for c in range(CH):
                        last = nc.tensor.matmul(c_bank[:, :], xt[p][:, c * S:(c + 1) * S],
                                                wc[p][:, c * DM:(c + 1) * DM], start=c == 0, stop=c == CH - 1)
                    last.then_inc(ev["c_done"], 1)
                if st.has(-2, B):
                    st.wait(ev["zst_out"], -2)
                    nc.tensor.matmul(y_bank[p][:, :], zst[:, :], lora_b[:, :], start=False, stop=True).then_inc(ev["x1_done"], 1)
                if st.has(-1, B):
                    st.wait(ev["c_out"], -1)
                    st.wait(ev["ct_out"], -2)
                    for c in range(CH):
                        last = nc.tensor.transpose(ct_bank[:, c * 128:(c + 1) * 128],
                                                   c_sb[q][:, c * 128:(c + 1) * 128], ident[:, :])
                    last.then_inc(ev["ct_put"], 1)
                if st.has(-2, B):
                    st.wait(ev["x1_out"], -2)
                    st.wait(ev["x1t_lo"], -3)
                    for c in range(CH):
                        last = nc.tensor.transpose(xt_bank[:, c * 128:(c + 1) * 128],
                                                   x1[p][:, c * 128:(c + 1) * 128], ident[:, :])
                    last.then_inc(ev["x1t_put"], 1)
                if st.has(-1, B):
                    if st.fixed and st.value == 1:
                        pe.wait_ge(s_w0, 16 * (CH + 1))
                    st.wait(ev["ct_out"], -1)
                    st.wait(ev["zs_out"], -3)
                    st.wait(ev["x1_out"], -3)
                    for c in range(CH):
                        last = nc.tensor.matmul(z_bank[q][:, 0:ZCOLS + NE], ct[q][:, c * 128:(c + 1) * 128],
                                                w0[:, c, DM:L0COLS], start=c == 0, stop=c == CH - 1)
                    last.then_inc(ev["z_put"], 1)
                    for c in range(CH):
                        last = nc.tensor.matmul(y_bank[q][:, :], ct[q][:, c * 128:(c + 1) * 128],
                                                w0[:, c, 0:DM], start=c == 0, stop=False)
                    last.then_inc(ev["y_put"], 1)

            run_steps(pe, 0, 2, B, END, body)

        @block.scalar
        def _(act):
            for s in mine["act"]:
                act.sem_inc(s, 1)
            act.wait_ge(s_prior, 1)
            nc.scalar.activation(lprior[:, :], prior[:, :], ACT.Ln, bias=eps_col[:, :]).then_inc(s_router, 1)
            act.wait_ge(s_sin, 1)
            nc.scalar.activation(sin[:, :, :], angle[:, :, :], ACT.Sin).then_inc(s_sin, 1)
            act.wait_ge(s_sin, 3)
            nc.scalar.activation(cos[:, :, :], turns[:, :, :], ACT.Sin).then_inc(s_sin, 1)

            def body(st):
                p, q = st.parity(), st.parity(-1)
                if st.has(-2, B):
                    st.wait(ev["zt_put"], -2)
                    st.wait(ev["x1_done"], -3)
                    nc.scalar.copy(zst[:, :], zt_bank[:, 0:S]).then_inc(ev["zst_out"], 1)
                if st.has(0, B):
                    st.wait(ev["c_done"], 0)
                    st.wait(ev["ct_put"], -2)
                    nc.scalar.copy(c_sb[p][:, :], c_bank[:, :]).then_inc(ev["c_out"], 1)
                if st.has(-1, B):
                    st.wait(ev["ct_put"], -1)
                    st.wait(ev["y_put"], -3)
                    nc.scalar.copy(ct[q][:, :], ct_bank[:, :]).then_inc(ev["ct_out"], 1)
                if st.has(-2, B):
                    st.wait(ev["x1t_put"], -2)
                    if not st.fixed or st.value >= 4:
                        st.wait_dma(s_st, -4, 2)
                    nc.scalar.copy(x1t[p][:, 0:CH * S], xt_bank[:, :]).then_inc(ev["x1t_hi"], 1)
                if st.has(0, AHEAD):
                    st.wait_dma(s_raw, 0)
                    nc.scalar.copy(w_hi[:, bass.ds(st.number(lambda v: v * WC), WC)], raw[p][:, :]).then_inc(ev["w_hi_a"], 1)
                if st.has(-1, B):
                    st.wait(ev["logit_out"], -1)
                    st.wait(ev["zs_out"], -2)
                    nc.scalar.activation(expl[:, :], logit[:, :], ACT.Exp, bias=ntop[:, :]).then_inc(ev["expl_out"], 1)

            run_steps(act, 0, 4, B, END, body)

        @block.gpsimd
        def _(pool):
            for s in mine["pool"]:
                pool.sem_inc(s, 1)
            nc.gpsimd.memset(ident[:, :], 0.0).then_inc(s_consts, 1)
            nc.gpsimd.memset(eps_col[:, :], PRIOR_EPS)
            pool.wait_ge(s_consts, 1)
            nc.gpsimd.affine_select(out=ident[:, :], in_=ident[:, :], compare_op=ALU.not_equal, fill=1.0,
                                    base=0, pattern=[[-1, 128]], channel_multiplier=1).then_inc(s_consts, 1)
            nc.gpsimd.iota(expert[:, :], pattern=[[1, NE]], base=0, channel_multiplier=0,
                           allow_small_or_imprecise_dtypes=True)
            nc.gpsimd.iota(tok[:, :], pattern=[[1, 1]], base=0, channel_multiplier=1,
                           allow_small_or_imprecise_dtypes=True)
            nc.gpsimd.iota(key_no[:, :], pattern=[[1, L]], base=0, channel_multiplier=0,
                           allow_small_or_imprecise_dtypes=True)
            nc.gpsimd.memset(mask[:, :, L:KEYS], 0.0).then_inc(s_consts, 1)
            pool.wait_ge(s_rows, 16 * 7)

            def body(st):
                p = st.parity()
                if st.has(0, AHEAD):
                    st.wait(ev["w_hi_a"], 0)
                    at = bass.ds(st.number(lambda v: v * WC), WC)
                    nc.gpsimd.tensor_tensor(w_lo[:, at], raw[p][:, :], w_hi[:, at].bitcast(F32),
                                            ALU.subtract).then_inc(ev["w_lo_a"], 1)
                if st.has(0, B):
                    st.wait_dma(s_xn, 0)
                    st.wait(ev["x1_out"], -2)
                    nc.gpsimd.tensor_tensor(xb[p][:, :], xn[p][:, :], bias[:, :], ALU.add).then_inc(ev["xb_out"], 1)

            run_steps(pool, 0, 2, B, END, body)

        @block.vector
        def _(dve):
            for s in mine["dve"]:
                dve.sem_inc(s, 1)
            count = [0]

            def chain(ins):
                count[0] += 1
                ins.then_inc(s_v, 1)
                dve.wait_ge(s_v, count[0])

            dve.wait_ge(s_consts, 3)
            dve.wait_ge(s_rows, 16 * 7)
            dve.sem_inc(s_prior, 1)
            nc.vector.tensor_copy(act_f[:, :], active[:, :])
            nc.vector.tensor_copy(seq_f[:, :], seq_i[:, :])
            nc.vector.tensor_scalar(norm_w[:, 0:D], norm_w[:, 0:D], SCALE, None, ALU.mult)
            chain(nc.vector.memset(times[:, :], 0.0))
            for a in range(NACT):
                chain(nc.vector.scalar_tensor_tensor(out=times[:, :], in0=expert[:, :], scalar=act_f[:, a:a + 1],
                                                     in1=times[:, :], op0=ALU.is_equal, op1=ALU.add))
            chain(nc.vector.tensor_scalar(unused[:, :], times[:, :], 0.0, MASKED, ALU.is_equal, ALU.mult))
            dve.wait_ge(s_router, 1)
            chain(nc.vector.tensor_tensor(lbias[:, :], lprior[:, :], router_b[:, :], ALU.add))
            chain(nc.vector.tensor_tensor(lbias[:, :], lbias[:, :], unused[:, :], ALU.add))

            def tables():
                half = D // 2
                chain(nc.vector.tensor_scalar(pos[:, :], seq_f[:, :], tok[:, :], None, ALU.add))
                pos_b = pos[:, :].unsqueeze(2).to_broadcast([128, B, half])
                invf_b = invf[:, :].unsqueeze(1).to_broadcast([128, B, half])
                chain(nc.vector.tensor_tensor(angle[:, :, :], pos_b, invf_b, ALU.mult))
                chain(nc.vector.tensor_scalar(turns[:, :, :], angle[:, :, :], 0.5 / PI, 0.25, ALU.mult, ALU.add))
                chain(nc.vector.tensor_scalar(turns[:, :, :], turns[:, :, :], ROUND_INT, -ROUND_INT, ALU.add, ALU.add))
                chain(nc.vector.scalar_tensor_tensor(out=cos[:, :, :], in0=turns[:, :, :], scalar=-TWO_PI_PARTS[0],
                                                     in1=angle[:, :, :], op0=ALU.mult, op1=ALU.add))
                for part in TWO_PI_PARTS[1:]:
                    chain(nc.vector.scalar_tensor_tensor(out=cos[:, :, :], in0=turns[:, :, :], scalar=-part,
                                                         in1=cos[:, :, :], op0=ALU.mult, op1=ALU.add))
                chain(nc.vector.tensor_scalar(turns[:, :, :], angle[:, :, :], 0.5 / PI, ROUND_INT, ALU.mult, ALU.add))
                chain(nc.vector.tensor_scalar(turns[:, :, :], turns[:, :, :], -ROUND_INT, None, ALU.add))
                for part in TWO_PI_PARTS:
                    chain(nc.vector.scalar_tensor_tensor(out=angle[:, :, :], in0=turns[:, :, :], scalar=-part,
                                                         in1=angle[:, :, :], op0=ALU.mult, op1=ALU.add))
                nc.vector.tensor_scalar(angle[:, :, :], angle[:, :, :], PI_IN, -PI_IN, ALU.min, ALU.max).then_inc(s_sin, 1)
                chain(nc.vector.tensor_scalar(turns[:, :, :], cos[:, :, :], PI / 2, PI_IN, ALU.add, ALU.min))
                nc.vector.tensor_scalar(turns[:, :, :], turns[:, :, :], -PI_IN, None, ALU.max).then_inc(s_sin, 1)
                key_b = key_no[:, :].unsqueeze(1).to_broadcast([128, B, L])
                seq_b = seq_f[:, :].unsqueeze(2).to_broadcast([128, B, L])
                chain(nc.vector.tensor_tensor(mask[:, :, 0:L], key_b, seq_b, ALU.is_ge))
                nc.vector.tensor_scalar(mask[:, :, 0:L], mask[:, :, 0:L], MASKED, None, ALU.mult).then_inc(s_tables, 1)
                dve.wait_ge(s_sin, 4)
                for k in range(2):
                    w1 = norm_w[:, k * D:k * D + half].unsqueeze(1).to_broadcast([128, B, half])
                    w2 = norm_w[:, k * D + half:(k + 1) * D].unsqueeze(1).to_broadcast([128, B, half])
                    at = 2 * D * k
                    nc.vector.tensor_tensor(rope[:, :, at:at + half], cos[:, :, :], w1, ALU.mult)
                    nc.vector.tensor_tensor(rope[:, :, at + half:at + D], cos[:, :, :], w2, ALU.mult)
                    chain(nc.vector.tensor_tensor(rope[:, :, at + D:at + D + half], sin[:, :, :], w2, ALU.mult))
                    last = nc.vector.tensor_scalar(rope[:, :, at + D:at + D + half], rope[:, :, at + D:at + D + half],
                                                   -1.0, None, ALU.mult)
                    last = nc.vector.tensor_tensor(rope[:, :, at + D + half:at + 2 * D], sin[:, :, :], w1, ALU.mult)
                last.then_inc(s_tables, 1)

            tables()
            s_self = sem("s_self")
            dve.sem_inc(s_self, 1)

            def body(st):
                p, q = st.parity(), st.parity(-1)
                if st.has(-2, B):
                    st.wait(ev["x1_done"], -2)
                    st.wait(ev["xb_out"], -2)
                    if not st.fixed or st.value >= 4:
                        st.wait_dma(s_st, -4, 2)
                    nc.vector.tensor_tensor(x1[p][:, :], y_bank[p][:, :], xb[p][:, :], ALU.add).then_inc(ev["x1_out"], 1)
                    st.wait(ev["x1t_hi"], -2)
                    nc.vector.tensor_tensor(x1t[p][:, CH * S:2 * CH * S], xt_bank[:, :],
                                            x1t[p][:, 0:CH * S].bitcast(F32), ALU.subtract).then_inc(ev["x1t_lo"], 1)
                if st.has(-1, B):
                    st.wait(ev["z_put"], -1)
                    st.wait(ev["expl_out"], -2)
                    nc.vector.tensor_tensor(logit[:, :], z_bank[q][:, ZCOLS:ZCOLS + NE], lbias[:, :],
                                            ALU.add).then_inc(v_step["a"], 1)
                    st.wait(v_step["a"], -1)
                    nc.vector.reduce_max(top[:, :], logit[:, :], AX).then_inc(v_step["b"], 1)
                    st.wait(v_step["b"], -1)
                    nc.vector.tensor_scalar(ntop[:, :], top[:, :], -1.0, None, ALU.mult).then_inc(ev["logit_out"], 1)
                    st.wait(ev["expl_out"], -1)
                    nc.vector.tensor_tensor(alpha[:, :], expl[:, :], times[:, :], ALU.mult).then_inc(v_step["c"], 1)
                    st.wait(v_step["c"], -1)
                    nc.vector.reduce_sum(total[:, :], alpha[:, :], AX).then_inc(v_step["d"], 1)
                    st.wait(v_step["d"], -1)
                    nc.vector.reciprocal(rtotal[:, :], total[:, :]).then_inc(v_step["e"], 1)
                    st.wait(v_step["e"], -1)
                    nc.vector.tensor_scalar(alpha[:, :], alpha[:, :], rtotal[:, :], LORA_SCALE, ALU.mult,
                                            ALU.mult).then_inc(v_step["f"], 1)
                    st.wait(v_step["f"], -1)
                    st.wait(ev["zt_put"], -2)
                    nc.vector.tensor_tensor(zs[:, :].rearrange("p (e r) -> p e r", r=RK),
                                            z_bank[q][:, 0:ZCOLS].rearrange("p (e r) -> p e r", r=RK),
                                            alpha[:, :].unsqueeze(2).to_broadcast([128, NE, RK]),
                                            ALU.mult).then_inc(ev["zs_out"], 1)

            v_step = {}
            for name in "abcdef":
                v_step[name] = sem(f"v_{name}")
                dve.sem_inc(v_step[name], 1)
            run_steps(dve, 0, 4, B, END, body)


def attention(nc, sem_ctx, s_spare, t, ident, w_hi, w_lo, attn, scratch):
    x1t_dram, _, rope_dram, mask_dram = scratch
    ctx = ExitStack()
    with ctx:
        def sb(name, shape, dt=F32):
            return ctx.enter_context(nc.sbuf_tensor(name, shape, dt))

        def sem(name):
            return sem_ctx.enter_context(nc.semaphore(name))

        two = range(2)
        raw = [sb(f"raw{p}", [128, WC]) for p in two]
        kv = [sb(f"kv{p}", [128, CT, 2 * D]) for p in two]
        x1t = [sb(f"x1ts{p}", [128, 2 * CH * S], F32R) for p in two]
        rope = [sb(f"rope{p}", [128, 4 * D]) for p in two]
        mask = [sb(f"mask{p}", [128, KEYS]) for p in two]
        qkv = sb("qkv", [128, WP])
        sq = sb("sq", [128, (G + 1) * D])
        ssum = sb("ssum", [128, G + 1])
        half_neg = sb("half_neg", [128, G + 1])
        rms = [sb(f"rms{p}", [128, G + 1]) for p in two]
        q_cos, q_sin, q_rot = (sb(n, [128, G * D]) for n in ("q_cos", "q_sin", "q_rot"))
        k_cos, k_sin, k_rot = (sb(n, [128, D]) for n in ("k_cos", "k_sin", "k_rot"))
        qt_hi, qt_lo = (sb(n, [128, G * S], F32R) for n in ("qt_hi", "qt_lo"))
        kt_hi, kt_lo = (sb(n, [128, KEYS], F32R) for n in ("kt_hi", "kt_lo"))
        v_hi = [sb(f"v_hi{p}", [128, KT, D], F32R) for p in two]
        v_lo = [sb(f"v_lo{p}", [128, KT, D], F32R) for p in two]
        score = [sb(f"score{p}", [128, KEYS]) for p in two]
        top = sb("top_score", [128, G])
        nbias = sb("nbias", [128, G])
        prob = [sb(f"prob{p}", [128, G, KEYS]) for p in two]
        psum_row = [sb(f"row_sum{p}", [128, G]) for p in two]
        rsum = sb("rsum", [128, G])
        rsum_b = sb("rsum_b", [128, G * S])
        pt_hi = [sb(f"pt_hi{p}", [128, G * S], F32R) for p in two]
        pt_lo = [sb(f"pt_lo{p}", [128, G * S], F32R) for p in two]
        o_sb = sb("o_sb", [128, G * S])
        o_hi, o_lo = (sb(n, [128, G * S], F32R) for n in ("o_hi", "o_lo"))

        slot = [ctx.enter_context(nc.psum_tensor(f"slot{p}", [128, 1024], F32)) for p in two]
        ring = [ctx.enter_context(nc.psum_tensor(f"ring{p}", [128, 512], F32)) for p in two]
        o_bank = ctx.enter_context(nc.psum_tensor("o_bank", [128, 512], F32))
        wo_bank = ctx.enter_context(nc.psum_tensor("wo_bank", [128, 512], F32))

        heads, tiles = range(G), range(KT)
        names = lambda stem, over: " ".join(f"{stem}{j}" for j in over)
        ev, mine = events(sem_ctx, nc, {
            "pe": f"proj rs_put q_put kc_put kn_put wo_done {names('s_put', heads)} {names('pt_put', tiles)} "
                  f"{names('pv', tiles)}",
            "act": f"qkv_out sq_out rs_out o_hi_out q_hi kc_hi kn_hi w_hi_out {names('exp', heads)} {names('pt_hi_out', tiles)}",
            "dve": f"ss_out q_sin_out k_parts k_sum o_mul o_lo_out q_lo kc_lo kn_lo rs acc {names('mx', heads)} "
                   f"{names('nb', heads)} {names('pt_lo_out', tiles)}",
            "pool": "ms rms_out q_cos_out q_sum v_hi_out v_out w_lo_out",
        })
        s_raw = [sem(f"s_raw{p}") for p in two]
        s_kv = [sem(f"s_kv{p}") for p in two]
        s_x1t = [sem(f"s_x1t{p}") for p in two]
        s_rope = [sem(f"s_rope{p}") for p in two]
        s_mask = [sem(f"s_mask{p}") for p in two]
        s_half, s_zero = sem("s_half"), sem("s_zero")

        block = ctx.enter_context(nc.Block())
        FIRST, LOOP0, LOOP1, END = -1, 2, STEPS - 2, STEPS + 2

        @block.sync
        def _(sp):
            def body(st):
                p, q = st.parity(), st.parity(1)
                if st.has(1, STEPS) and not (st.fixed and st.value + 1 + AHEAD > STEPS):
                    chunk = st.number(lambda v: (v + 1 + AHEAD) & (STEPS - 1))
                    st.wait(ev["w_lo_out"], -1)
                    st.hold()
                    sp.dma_start(raw[q][:, :], flat(t["weights"][bass.ds(chunk, 1)])).then_inc(s_raw[q], 16)
                if st.has(2, STEPS):
                    b = st.number(lambda v: (v + 2) & (B - 1))
                    hk = st.number(lambda v: (v + 2) >> 3 & (HK - 1))
                    st.wait(ev["proj"], 0)
                    st.hold()
                    sp.dma_start(x1t[p][:, :].bitcast(F32), flat(x1t_dram[bass.ds(b, 1)])).then_inc(s_x1t[p], 16)
                    st.wait(ev["k_parts"], 0)
                    st.wait(ev["q_sin_out"], 0)
                    st.wait(ev["q_cos_out"], 0)
                    st.hold()
                    sp.dma_start(rope[p][:, :], flat(rope_dram[bass.ds(b, 1)])).then_inc(s_rope[p], 16)
                if st.has(1, STEPS):
                    b = st.number(lambda v: (v + 1) & (B - 1))
                    st.wait(ev["mx3"], -1)
                    st.hold()
                    sp.dma_start(mask[q][:, :], flat(mask_dram[bass.ds(b, 1)])).then_inc(s_mask[q], 16)
                if st.has(2, STEPS):
                    b = st.number(lambda v: (v + 2) & (B - 1))
                    _, pages = nc.values_load_multi_w_load_instructions(
                        t["block_table"][bass.ds(b, 1), :], engines=[sp.engine], min_val=0, max_val=PAGES - 1)
                    st.wait(ev["kc_put"], 0)
                    st.wait(ev["v_out"], 0)
                    st.hold()
                    for j in range(NPP):
                        sp.dma_start(kv[p][PSIZE * (j % PPT):PSIZE * (j % PPT + 1), j // PPT, :],
                                     t["kv"][bass.ds(hk, 1), bass.ds(pages[j], 1)].rearrange("a b t n -> (a b t) n")
                                     ).then_inc(s_kv[p], 16)

            run_steps(sp, FIRST - 1, LOOP0, LOOP1, END, body, s_spare)

        @block.tensor
        def _(pe):
            for s in mine["pe"]:
                pe.sem_inc(s, 1)

            def body(st):
                i0, i1 = st.parity(), st.parity(1)
                t_bank = lambda use: ring[st.parity(use)]
                if st.has(1, STEPS):
                    at = st.number(lambda v: ((v + 1) >> 3 & 1) * WCOLS)
                    st.wait_dma(s_x1t, 1)
                    if not (st.fixed and st.value < 0):
                        st.wait(ev["w_hi_out"], -1)
                        st.wait(ev["w_lo_out"], -1)
                    st.wait(ev["mx2"], -1)
                    xh = [x1t[i1][:, c * S:(c + 1) * S] for c in range(CH)]
                    xl = [x1t[i1][:, (CH + c) * S:(CH + c + 1) * S] for c in range(CH)]
                    wh, wl = w_hi[:, bass.ds(at, CH * WP)], w_lo[:, bass.ds(at, CH * WP)]
                    for lo, hi in ((0, G * D), (G * D, WP)):
                        last = split3(nc, slot[i0][:, lo:hi],
                                      [((xh[c], xl[c]), (wh[:, c * WP + lo:c * WP + hi], wl[:, c * WP + lo:c * WP + hi]))
                                       for c in range(CH)], True, True)
                    last.then_inc(ev["proj"], 1)

                def ring_free(usual, past_end):
                    if st.has(0, STEPS):
                        st.wait(ev[usual], 0)
                    else:
                        st.wait(ev[past_end], -2)

                def values_transpose(kt):
                    prev = ev["rs_out"] if kt == 1 else ev[f"pt_lo_out{kt - 2}"] if kt else None
                    if kt == 0:
                        st.wait(ev["exp3"], -1)
                        ring_free("kn_lo", "pt_lo_out3")
                    else:
                        st.wait(prev, -1)
                    bank = t_bank(1 + kt)
                    for h in heads:
                        last = nc.tensor.transpose(bank[:, h * S:(h + 1) * S],
                                                   prob[i1][:, h, kt * 128:(kt + 1) * 128], ident[:, :])
                    last.then_inc(ev[f"pt_put{kt}"], 1)

                def values_product(kt):
                    st.wait(ev[f"pt_lo_out{kt}"], -1)
                    if kt == 0:
                        st.wait(ev["v_out"], -1)
                        st.wait(ev["o_mul"], -2)
                    u = st.parity(-1 + kt)
                    split3(nc, o_bank[:, :], [((v_hi[i1][:, kt, :], v_lo[i1][:, kt, :]), (pt_hi[u][:, :], pt_lo[u][:, :]))],
                           kt == 0, kt == KT - 1).then_inc(ev[f"pv{kt}"], 1)

                def scores(h):
                    if h == 0:
                        st.wait(ev["q_lo"], 0)
                        st.wait(ev["kc_lo"], 0)
                        st.wait(ev["kn_lo"], 0)
                    if h == 1:
                        if st.has(1, STEPS):
                            st.wait(ev["sq_out"], 1)
                        else:
                            st.wait(ev["mx2"], -1)
                    else:
                        st.wait(ev["mx3" if h == 0 else f"mx{h - 2}"], -1 if h == 0 else 0)
                    bank = slot[st.parity(1 + h)]
                    qh, ql = qt_hi[:, h * S:(h + 1) * S], qt_lo[:, h * S:(h + 1) * S]
                    for a, k, first, final in ((qh, kt_hi, True, False), (qh, kt_lo, False, False), (ql, kt_hi, False, True)):
                        nc.tensor.matmul(bank[:, 0:L], a, k[:, 0:L], start=first, stop=final)
                        last = nc.tensor.matmul(bank[:, L:KEYS], a, k[:, L:KEYS], start=first, stop=final)
                    last.then_inc(ev[f"s_put{h}"], 1)

                if st.has(-1, STEPS):
                    st.wait(ev["rs"], -1)
                    ring_free("kc_lo", "pt_lo_out4")
                    for h in heads:
                        last = nc.tensor.transpose(t_bank(0)[:, h * S:(h + 1) * S],
                                                   rsum[:, h:h + 1].to_broadcast([128, 128]), ident[:, :])
                    last.then_inc(ev["rs_put"], 1)
                    values_transpose(0)
                if st.has(-2, STEPS):
                    at = st.number(lambda v: ((v - 2) >> 3 & 1) * WCOLS + CH * WP)
                    st.wait(ev["o_lo_out"], -2)
                    st.wait(ev["acc"], -3)
                    wh, wl = w_hi[:, bass.ds(at, G * DM)], w_lo[:, bass.ds(at, G * DM)]
                    split3(nc, wo_bank[:, :],
                           [((o_hi[:, h * S:(h + 1) * S], o_lo[:, h * S:(h + 1) * S]),
                             (wh[:, h * DM:(h + 1) * DM], wl[:, h * DM:(h + 1) * DM])) for h in heads],
                           True, True).then_inc(ev["wo_done"], 1)
                for u in range(G - 1):
                    if st.has(-1, STEPS):
                        values_transpose(u + 1)
                    if st.has(0, STEPS):
                        scores(u)
                    if st.has(-1, STEPS):
                        values_product(u)
                if st.has(-1, STEPS):
                    values_transpose(KT - 1)
                if st.has(0, STEPS):
                    scores(G - 1)
                if st.has(1, STEPS):
                    st.wait(ev["q_sum"], 1)
                    st.wait(ev["pt_lo_out3"], -1)
                    for h in heads:
                        last = nc.tensor.transpose(t_bank(6)[:, h * S:(h + 1) * S], q_rot[:, h * D:(h + 1) * D], ident[:, :])
                    last.then_inc(ev["q_put"], 1)
                    st.wait_dma(s_kv, 1, NPP)
                    st.wait(ev["pt_lo_out4"], -1)
                    for c in range(CT):
                        last = nc.tensor.transpose(t_bank(7)[:, c * 128:(c + 1) * 128], kv[i1][:, c, 0:D], ident[:, :])
                    last.then_inc(ev["kc_put"], 1)
                if st.has(-1, STEPS):
                    values_product(KT - 2)
                    values_product(KT - 1)
                if st.has(1, STEPS):
                    st.wait(ev["k_sum"], 1)
                    st.wait(ev["q_lo"], 1)
                    nc.tensor.transpose(t_bank(8)[:, 0:S], k_rot[:, :], ident[:, :]).then_inc(ev["kn_put"], 1)

            run_steps(pe, FIRST, LOOP0, LOOP1, END, body)

        @block.scalar
        def _(act):
            for s in mine["act"]:
                act.sem_inc(s, 1)

            def body(st):
                i0, i1 = st.parity(), st.parity(1)
                t_bank = lambda use: ring[st.parity(use)]

                def probs_hi(kt):
                    u = st.parity(-1 + kt)
                    st.wait(ev[f"pt_put{kt}"], -1)
                    st.wait(ev[f"pv{kt - 2}" if kt >= 2 else f"pv{kt + 3}"], -1 if kt >= 2 else -2)
                    nc.scalar.copy(pt_hi[u][:, :], t_bank(1 + kt)[:, :]).then_inc(ev[f"pt_hi_out{kt}"], 1)

                if st.has(-2, STEPS):
                    st.wait(ev["o_mul"], -2)
                    st.wait(ev["wo_done"], -3)
                    nc.scalar.copy(o_hi[:, :], o_sb[:, :]).then_inc(ev["o_hi_out"], 1)
                if st.has(0, STEPS) and not (st.fixed and st.value + AHEAD >= STEPS):
                    st.wait_dma(s_raw, 0)
                    st.wait(ev["proj"], 0)
                    st.wait(ev["wo_done"], -3)
                    at = st.number(lambda v: ((v + AHEAD) >> 3 & 1) * WCOLS + ((v + AHEAD) & (B - 1)) * WC)
                    nc.scalar.copy(w_hi[:, bass.ds(at, WC)], raw[i0][:, :]).then_inc(ev["w_hi_out"], 1)
                elif st.fixed and 0 <= st.value < STEPS:
                    act.sem_inc(ev["w_hi_out"], 1)
                if st.has(1, STEPS):
                    st.wait(ev["proj"], 1)
                    st.wait(ev["q_cos_out"], 0)
                    st.wait(ev["q_sin_out"], 0)
                    st.wait(ev["k_parts"], 0)
                    st.wait(ev["v_out"], 0)
                    nc.scalar.copy(qkv[:, :], slot[i0][:, 0:WP]).then_inc(ev["qkv_out"], 1)
                    st.wait(ev["ss_out"], 0)
                    nc.scalar.activation(sq[:, :], slot[i0][:, 0:(G + 1) * D], ACT.Square).then_inc(ev["sq_out"], 1)
                if st.has(-1, STEPS):
                    st.wait(ev["rs_put"], -1)
                    st.wait(ev["o_mul"], -2)
                    nc.scalar.copy(rsum_b[:, :], t_bank(0)[:, :]).then_inc(ev["rs_out"], 1)
                    probs_hi(0)

                def exps(h):
                    st.wait(ev[f"nb{h}"], 0)
                    if h == 0:
                        st.wait(ev["pt_put4"], -2)
                        st.wait(ev["rs"], -2)
                    nc.scalar.activation(prob[i0][:, h, :], score[h % 2][:, :], ACT.Exp, bias=nbias[:, h:h + 1],
                                         scale=rms[i0][:, h:h + 1],
                                         accum_out=psum_row[i0][:, h:h + 1]).then_inc(ev[f"exp{h}"], 1)

                for kt in range(1, KT):
                    if st.has(-1, STEPS):
                        probs_hi(kt)
                    if st.has(0, STEPS) and kt > 1:
                        exps(kt - 2)
                if st.has(1, STEPS):
                    st.wait(ev["q_put"], 1)
                    st.wait(ev["s_put3"], 0)
                    nc.scalar.copy(qt_hi[:, :], t_bank(6)[:, :]).then_inc(ev["q_hi"], 1)
                if st.has(0, STEPS):
                    exps(G - 1)
                if st.has(1, STEPS):
                    st.wait(ev["kc_put"], 1)
                    nc.scalar.copy(kt_hi[:, 0:L], t_bank(7)[:, :]).then_inc(ev["kc_hi"], 1)
                    st.wait(ev["kn_put"], 1)
                    nc.scalar.copy(kt_hi[:, L:KEYS], t_bank(8)[:, 0:S]).then_inc(ev["kn_hi"], 1)

            run_steps(act, FIRST, LOOP0, LOOP1, END, body)

        @block.gpsimd
        def _(pool):
            nc.gpsimd.memset(half_neg[:, :], -0.5).then_inc(s_half, 1)
            pool.wait_ge(s_half, 1)
            for s in mine["pool"]:
                pool.sem_inc(s, 1)

            def body(st):
                i0, i1 = st.parity(), st.parity(1)
                if st.has(1, STEPS):
                    st.wait(ev["qkv_out"], 1)
                    st.wait_dma(s_rope, 1)
                    nc.gpsimd.tensor_tensor(q_cos[:, :].rearrange("p (h d) -> p h d", h=G),
                                            qkv[:, 0:G * D].rearrange("p (h d) -> p h d", h=G),
                                            rope[i1][:, 0:D].unsqueeze(1).to_broadcast([128, G, D]),
                                            ALU.mult).then_inc(ev["q_cos_out"], 1)
                    st.wait(ev["ss_out"], 1)
                    st.wait(ev["exp3"], -1)
                    st.wait(ev["nb3"], -1)
                    st.hold()
                    nc.gpsimd.tensor_scalar(rms[i1][:, :], ssum[:, :], 1.0 / D, NORM_EPS, ALU.mult, ALU.add).then_inc(ev["ms"], 1)
                    st.wait(ev["ms"], 1)
                    nc.gpsimd.tensor_tensor(rms[i1][:, :], rms[i1][:, :], half_neg[:, :], ALU.pow).then_inc(ev["rms_out"], 1)
                    st.wait(ev["q_sin_out"], 1)
                    st.wait(ev["q_put"], 0)
                    nc.gpsimd.tensor_tensor(q_rot[:, :], q_cos[:, :], q_sin[:, :], ALU.add).then_inc(ev["q_sum"], 1)
                if st.has(0, STEPS) and not (st.fixed and st.value + AHEAD >= STEPS):
                    st.wait(ev["w_hi_out"], 0)
                    at = st.number(lambda v: ((v + AHEAD) >> 3 & 1) * WCOLS + ((v + AHEAD) & (B - 1)) * WC)
                    nc.gpsimd.tensor_tensor(w_lo[:, bass.ds(at, WC)], raw[i0][:, :],
                                            w_hi[:, bass.ds(at, WC)].bitcast(F32), ALU.subtract).then_inc(ev["w_lo_out"], 1)
                elif st.fixed and 0 <= st.value < STEPS:
                    pool.sem_inc(ev["w_lo_out"], 1)
                if st.has(1, STEPS):
                    st.wait_dma(s_kv, 1, NPP)
                    st.wait(ev["pv4"], -1)
                    st.hold()
                    nc.gpsimd.tensor_copy(v_hi[i1][:, 0:CT, :], kv[i1][:, :, D:2 * D])
                    nc.gpsimd.tensor_copy(v_hi[i1][:, CT, :], qkv[:, WP - D:WP]).then_inc(ev["v_hi_out"], 1)
                    st.wait(ev["v_hi_out"], 1)
                    nc.gpsimd.tensor_tensor(v_lo[i1][:, 0:CT, :], kv[i1][:, :, D:2 * D],
                                            v_hi[i1][:, 0:CT, :].bitcast(F32), ALU.subtract)
                    nc.gpsimd.tensor_tensor(v_lo[i1][:, CT, :], qkv[:, WP - D:WP],
                                            v_hi[i1][:, CT, :].bitcast(F32), ALU.subtract).then_inc(ev["v_out"], 1)

            run_steps(pool, FIRST, LOOP0, LOOP1, END, body, s_spare)

        @block.vector
        def _(dve):
            for s in mine["dve"]:
                dve.sem_inc(s, 1)
            nc.vector.memset(attn[:, :], 0.0).then_inc(s_zero, 1)
            dve.wait_ge(s_zero, 1)

            def body(st):
                i0, i1 = st.parity(), st.parity(1)
                t_bank = lambda use: ring[st.parity(use)]

                def probs_lo(kt):
                    u = st.parity(-1 + kt)
                    st.wait(ev[f"pt_hi_out{kt}"], -1)
                    nc.vector.tensor_tensor(pt_lo[u][:, :], t_bank(1 + kt)[:, :], pt_hi[u][:, :].bitcast(F32),
                                            ALU.subtract).then_inc(ev[f"pt_lo_out{kt}"], 1)

                if st.has(-2, STEPS):
                    st.wait(ev["pv4"], -2)
                    st.wait(ev["rs_out"], -2)
                    st.wait(ev["o_lo_out"], -3)
                    nc.vector.tensor_tensor(o_sb[:, :], o_bank[:, :], rsum_b[:, :], ALU.mult).then_inc(ev["o_mul"], 1)
                if st.has(-1, STEPS):
                    st.wait(ev["exp3"], -1)
                    st.wait(ev["rs_put"], -2)
                    nc.vector.reciprocal(rsum[:, :], psum_row[i1][:, :]).then_inc(ev["rs"], 1)
                if st.has(-2, STEPS):
                    st.wait(ev["o_hi_out"], -2)
                    nc.vector.tensor_tensor(o_lo[:, :], o_sb[:, :], o_hi[:, :].bitcast(F32), ALU.subtract).then_inc(ev["o_lo_out"], 1)
                if st.has(1, STEPS):
                    st.wait_dma(s_rope, 1)
                    st.wait(ev["qkv_out"], 1)
                    st.wait(ev["q_sum"], 0)
                    qs = q_sin[:, :].rearrange("p (h d) -> p h d", h=G)
                    qp = qkv[:, 0:G * D].rearrange("p (h d) -> p h d", h=G)
                    half = D // 2
                    for lo, hi in ((0, half), (half, 0)):
                        last = nc.vector.tensor_tensor(qs[:, :, lo:lo + half], qp[:, :, hi:hi + half],
                                                       rope[i1][:, D + lo:D + lo + half].unsqueeze(1).to_broadcast([128, G, half]),
                                                       ALU.mult)
                    last.then_inc(ev["q_sin_out"], 1)
                    st.wait(ev["sq_out"], 1)
                    nc.vector.reduce_sum(ssum[:, :], sq[:, :].rearrange("p (h d) -> p h d", h=G + 1), AX).then_inc(ev["ss_out"], 1)
                if st.has(-1, STEPS):
                    probs_lo(0)
                if st.has(-2, STEPS):
                    b = st.number(lambda v: ((v - 2) & (B - 1)) * DM)
                    st.wait(ev["wo_done"], -2)
                    at = attn[:, bass.ds(b, DM)]
                    nc.vector.tensor_tensor(at, wo_bank[:, :], at, ALU.add).then_inc(ev["acc"], 1)
                for h in heads:
                    if st.has(-1, STEPS):
                        probs_lo(h + 1)
                    if st.has(0, STEPS):
                        if h == 0:
                            st.wait_dma(s_mask, 0)
                        st.wait(ev[f"exp{h - 2}" if h >= 2 else f"exp{h + 2}"], 0 if h >= 2 else -1)
                        st.wait(ev[f"s_put{h}"], 0)
                        st.hold()
                        nc.vector.tensor_tensor_reduce(out=score[h % 2][:, :], in0=slot[st.parity(1 + h)][:, 0:KEYS],
                                                       in1=mask[i0][:, :], scale=1.0, scalar=LOWEST, op0=ALU.add,
                                                       op1=ALU.max, accum_out=top[:, h:h + 1]).then_inc(ev[f"mx{h}"], 1)
                        st.wait(ev[f"mx{h}"], 0)
                        nc.vector.tensor_scalar(nbias[:, h:h + 1], top[:, h:h + 1], rms[i0][:, h:h + 1], -1.0,
                                                ALU.mult, ALU.mult).then_inc(ev[f"nb{h}"], 1)
                    if h == 0 and st.has(1, STEPS):
                        kc = qkv[:, G * D:(G + 1) * D]
                        rk = rms[i1][:, G:G + 1]
                        st.wait(ev["rms_out"], 1)
                        nc.vector.scalar_tensor_tensor(out=k_cos[:, :], in0=kc, scalar=rk, in1=rope[i1][:, 2 * D:3 * D],
                                                       op0=ALU.mult, op1=ALU.mult)
                        for lo, hi in ((0, half), (half, 0)):
                            last = nc.vector.scalar_tensor_tensor(out=k_sin[:, lo:lo + half], in0=kc[:, hi:hi + half], scalar=rk,
                                                                  in1=rope[i1][:, 3 * D + lo:3 * D + lo + half],
                                                                  op0=ALU.mult, op1=ALU.mult)
                        last.then_inc(ev["k_parts"], 1)
                    if h == 1 and st.has(1, STEPS):
                        st.wait(ev["k_parts"], 1)
                        st.wait(ev["kn_put"], 0)
                        nc.vector.tensor_tensor(k_rot[:, :], k_cos[:, :], k_sin[:, :], ALU.add).then_inc(ev["k_sum"], 1)
                if st.has(1, STEPS):
                    st.wait(ev["q_hi"], 1)
                    nc.vector.tensor_tensor(qt_lo[:, :], t_bank(6)[:, :], qt_hi[:, :].bitcast(F32), ALU.subtract).then_inc(ev["q_lo"], 1)
                    st.wait(ev["kc_hi"], 1)
                    nc.vector.tensor_tensor(kt_lo[:, 0:L], t_bank(7)[:, :], kt_hi[:, 0:L].bitcast(F32), ALU.subtract).then_inc(ev["kc_lo"], 1)
                    st.wait(ev["kn_hi"], 1)
                    nc.vector.tensor_tensor(kt_lo[:, L:KEYS], t_bank(8)[:, 0:S], kt_hi[:, L:KEYS].bitcast(F32),
                                            ALU.subtract).then_inc(ev["kn_lo"], 1)

            run_steps(dve, FIRST, LOOP0, LOOP1, END, body, s_spare)


def last_layer(nc, sem_ctx, s_spare, t, ident, attn, scratch, out):
    _, x1_dram, _, _ = scratch
    ctx = ExitStack()
    with ctx:
        def sb(name, shape, dt=F32):
            return ctx.enter_context(nc.sbuf_tensor(name, shape, dt))

        def sem(name):
            return sem_ctx.enter_context(nc.semaphore(name))

        two = range(2)
        had = sb("had", [128, CH * DM])
        had_r = sb("had_r", [128, CH * DM], F32R)
        w8 = sb("w8", [128, CH * DM])
        w8_hi, w8_lo = (sb(n, [128, CH * DM], F32R) for n in ("w8_hi", "w8_lo"))
        scales = sb("scales", [128, DM])
        bias = sb("bias1", [128, DM])
        a_st = [sb(f"a_st{p}", [128, DM]) for p in two]
        at_hi = [sb(f"at_hi{p}", [128, CH * S], F32R) for p in two]
        at_lo = [sb(f"at_lo{p}", [128, CH * S], F32R) for p in two]
        xh = [sb(f"xh{p}", [128, DM]) for p in two]
        amax, sx, rsx = ([sb(f"{n}{p}", [128, 1]) for p in two] for n in ("amax", "sx", "rsx"))
        xabs = sb("xabs", [128, DM])
        v = [sb(f"v{p}", [128, DM]) for p in two]
        step = [sb(f"step{p}", [128, DM]) for p in two]
        qv = [sb(f"qv{p}", [128, DM]) for p in two]
        qt = [sb(f"qt{p}", [128, CH * S], F32R) for p in two]
        x1 = [sb(f"x1f{p}", [128, DM]) for p in two]
        x1b = [sb(f"x1b{p}", [128, DM]) for p in two]
        y = [sb(f"y{p}", [128, DM]) for p in two]
        res = [sb(f"res{p}", [128, DM]) for p in two]
        bank = {n: [ctx.enter_context(nc.psum_tensor(f"{n}{p}", [128, 512], F32)) for p in two]
                for n in ("a_bank", "h_bank", "q_bank", "f_bank")}

        ev, mine = events(sem_ctx, nc, {
            "pe": "at_put rot qt_put ffn",
            "act": "at_hi_out abs_out scaled qt_out",
            "dve": "at_lo_out xh_out amax_out sx_out rsx_out expo step_out y_out",
            "pool": "a_out q_add q_out x1b_out res_out",
        })
        s_load, s_conv = sem("s_load"), sem("s_conv")
        s_x1 = [sem(f"s_x1f{p}") for p in two]
        s_out = [sem(f"s_out{p}") for p in two]
        block = ctx.enter_context(nc.Block())
        END = B + 2

        @block.sync
        def _(sp):
            sp.dma_start(had[:, :], t["hadamard"]).then_inc(s_load, 16)
            sp.dma_start(w8[:, :], t["w8"]).then_inc(s_load, 16)
            sp.dma_start(scales[:, :], t["scales"].partition_broadcast(128)).then_inc(s_load, 16)
            sp.dma_start(bias[:, :], t["bias"].partition_broadcast(128)).then_inc(s_load, 16)

            def body(st):
                p = st.parity()
                if st.has(0, B):
                    st.wait(ev["x1b_out"], -2)
                    st.hold()
                    sp.dma_start(x1[p][:, :], flat(x1_dram[bass.ds(st.value, 1)])).then_inc(s_x1[p], 16)
                if st.has(-2, B):
                    st.wait(ev["res_out"], -2)
                    st.hold()
                    sp.dma_start(flat(out[bass.ds(st.number(lambda i: i - 2), 1)]), res[p][:, :]).then_inc(s_out[p], 16)

            run_steps(sp, 0, 2, B, END, body, s_spare)
            for p in two:
                sp.wait_ge(s_out[p], 16 * B // 2)

        @block.tensor
        def _(pe):
            for s in mine["pe"]:
                pe.sem_inc(s, 1)

            def body(st):
                p, q = st.parity(), st.parity(-1)
                if st.has(0, B):
                    st.wait(ev["a_out"], 0)
                    st.wait(ev["at_lo_out"], -2)
                    for c in range(CH):
                        last = nc.tensor.transpose(bank["a_bank"][p][:, c * 128:(c + 1) * 128],
                                                   a_st[p][:, c * 128:(c + 1) * 128], ident[:, :])
                    last.then_inc(ev["at_put"], 1)
                if st.has(-1, B):
                    st.wait(ev["q_out"], -1)
                    st.wait(ev["qt_out"], -3)
                    for c in range(CH):
                        last = nc.tensor.transpose(bank["q_bank"][q][:, c * 128:(c + 1) * 128],
                                                   qv[q][:, c * 128:(c + 1) * 128], ident[:, :])
                    last.then_inc(ev["qt_put"], 1)
                if st.has(0, B):
                    if st.fixed and st.value == 0:
                        pe.wait_ge(s_conv, 3)
                    st.wait(ev["at_lo_out"], 0)
                    st.wait(ev["xh_out"], -2)
                    for c in range(CH):
                        h = had_r[:, c * DM:(c + 1) * DM]
                        nc.tensor.matmul(bank["h_bank"][p][:, :], at_hi[p][:, c * S:(c + 1) * S], h, start=c == 0, stop=False)
                        last = nc.tensor.matmul(bank["h_bank"][p][:, :], at_lo[p][:, c * S:(c + 1) * S], h,
                                                start=False, stop=c == CH - 1)
                    last.then_inc(ev["rot"], 1)
                if st.has(-1, B):
                    st.wait(ev["qt_out"], -1)
                    st.wait(ev["y_out"], -3)
                    for c in range(CH):
                        a = qt[q][:, c * S:(c + 1) * S]
                        nc.tensor.matmul(bank["f_bank"][q][:, :], a, w8_hi[:, c * DM:(c + 1) * DM], start=c == 0, stop=False)
                        last = nc.tensor.matmul(bank["f_bank"][q][:, :], a, w8_lo[:, c * DM:(c + 1) * DM],
                                                start=False, stop=c == CH - 1)
                    last.then_inc(ev["ffn"], 1)

            run_steps(pe, 0, 2, B, END, body)

        @block.scalar
        def _(act):
            for s in mine["act"]:
                act.sem_inc(s, 1)
            act.wait_ge(s_load, 64)
            nc.scalar.copy(had_r[:, :], had[:, :]).then_inc(s_conv, 1)
            nc.scalar.copy(w8_hi[:, :], w8[:, :]).then_inc(s_conv, 1)

            def body(st):
                p, q = st.parity(), st.parity(-1)
                if st.has(0, B):
                    st.wait(ev["at_put"], 0)
                    st.wait(ev["rot"], -2)
                    nc.scalar.copy(at_hi[p][:, :], bank["a_bank"][p][:, :]).then_inc(ev["at_hi_out"], 1)
                if st.has(-1, B):
                    st.wait(ev["qt_put"], -1)
                    st.wait(ev["ffn"], -3)
                    nc.scalar.copy(qt[q][:, :], bank["q_bank"][q][:, :]).then_inc(ev["qt_out"], 1)
                if st.has(0, B):
                    st.wait(ev["xh_out"], 0)
                    st.wait(ev["amax_out"], -1)
                    nc.scalar.activation(xabs[:, :], xh[p][:, :], ACT.Abs).then_inc(ev["abs_out"], 1)
                    st.wait(ev["rsx_out"], 0)
                    st.wait(ev["q_add"], -2)
                    nc.scalar.activation(v[p][:, :], xh[p][:, :], ACT.Copy, scale=rsx[p][:, :]).then_inc(ev["scaled"], 1)

            run_steps(act, 0, 2, B, END, body)

        @block.vector
        def _(dve):
            for s in mine["dve"]:
                dve.sem_inc(s, 1)
            dve.wait_ge(s_conv, 2)
            nc.vector.tensor_tensor(w8_lo[:, :], w8[:, :], w8_hi[:, :].bitcast(F32), ALU.subtract).then_inc(s_conv, 1)

            def body(st):
                p, q = st.parity(), st.parity(-1)
                if st.has(0, B):
                    st.wait(ev["at_hi_out"], 0)
                    nc.vector.tensor_tensor(at_lo[p][:, :], bank["a_bank"][p][:, :], at_hi[p][:, :].bitcast(F32),
                                            ALU.subtract).then_inc(ev["at_lo_out"], 1)
                    st.wait(ev["rot"], 0)
                    st.wait(ev["scaled"], -2)
                    nc.vector.tensor_scalar(xh[p][:, :], bank["h_bank"][p][:, :], DM ** -0.5, None, ALU.mult).then_inc(ev["xh_out"], 1)
                    st.wait(ev["abs_out"], 0)
                    nc.vector.reduce_max(amax[p][:, :], xabs[:, :], AX).then_inc(ev["amax_out"], 1)
                    st.wait(ev["amax_out"], 0)
                    nc.vector.tensor_scalar(sx[p][:, :], amax[p][:, :], 1.0 / FP8_MAX, None, ALU.mult).then_inc(ev["sx_out"], 1)
                    st.wait(ev["sx_out"], 0)
                    nc.vector.reciprocal(rsx[p][:, :], sx[p][:, :]).then_inc(ev["rsx_out"], 1)
                if st.has(-1, B):
                    st.wait(ev["ffn"], -1)
                    st.wait(ev["res_out"], -3)
                    nc.vector.scalar_tensor_tensor(out=y[q][:, :], in0=bank["f_bank"][q][:, :], scalar=sx[q][:, :],
                                                   in1=scales[:, :], op0=ALU.mult, op1=ALU.mult).then_inc(ev["y_out"], 1)
                if st.has(0, B):
                    st.wait(ev["scaled"], 0)
                    st.wait(ev["q_out"], -2)
                    nc.vector.tensor_scalar(step[p][:, :].bitcast(U32), v[p][:, :].bitcast(U32), EXP_BITS, None,
                                            ALU.bitwise_and).then_inc(ev["expo"], 1)
                    st.wait(ev["expo"], 0)
                    nc.vector.tensor_scalar(step[p][:, :], step[p][:, :], MIN_E4M3, ROUND_E4M3, ALU.max,
                                            ALU.mult).then_inc(ev["step_out"], 1)

            run_steps(dve, 0, 2, B, END, body)

        @block.gpsimd
        def _(pool):
            for s in mine["pool"]:
                pool.sem_inc(s, 1)
            pool.wait_ge(s_load, 64)

            def body(st):
                p, q = st.parity(), st.parity(-1)
                if st.has(0, B):
                    st.wait(ev["at_put"], -2)
                    st.hold()
                    nc.gpsimd.tensor_copy(a_st[p][:, :], attn[:, bass.ds(st.number(lambda i: i * DM), DM)]).then_inc(ev["a_out"], 1)
                    st.wait_dma(s_x1, 0)
                    st.wait(ev["res_out"], -2)
                    nc.gpsimd.tensor_tensor(x1b[p][:, :], x1[p][:, :], bias[:, :], ALU.add).then_inc(ev["x1b_out"], 1)
                if st.has(-1, B):
                    st.wait(ev["y_out"], -1)
                    if not st.fixed or st.value >= 3:
                        st.wait_dma(s_out, -3)
                    nc.gpsimd.tensor_tensor(res[q][:, :], y[q][:, :], x1b[q][:, :], ALU.add).then_inc(ev["res_out"], 1)
                if st.has(0, B):
                    st.wait(ev["step_out"], 0)
                    nc.gpsimd.tensor_tensor(v[p][:, :], v[p][:, :], step[p][:, :], ALU.add).then_inc(ev["q_add"], 1)
                    st.wait(ev["q_add"], 0)
                    st.wait(ev["qt_put"], -2)
                    nc.gpsimd.tensor_tensor(qv[p][:, :], v[p][:, :], step[p][:, :], ALU.subtract).then_inc(ev["q_out"], 1)

            run_steps(pool, 0, 4, B, END, body, s_spare)


def build(nc, t, out):
    scratch = (
        nc.dram_tensor("x1t_scratch", (B, 128, 2 * CH * S), F32, kind="Internal").ap(),
        nc.dram_tensor("x1_scratch", (B, S, DM), F32, kind="Internal").ap(),
        nc.dram_tensor("rope_scratch", (B, 128, 4 * D), F32, kind="Internal").ap(),
        nc.dram_tensor("mask_scratch", (B, 128, KEYS), F32, kind="Internal").ap(),
    )
    with ExitStack() as sem_ctx, nc.sbuf_tensor("ident", [128, 128], F32) as ident, nc.sbuf_tensor("attn", [128, B * DM], F32) as attn:
        s_spare = sem_ctx.enter_context(nc.semaphore("s_spare"))
        with (nc.sbuf_tensor("w_hi", [128, 2 * WCOLS], F32R) as w_hi,
              nc.sbuf_tensor("w_lo", [128, 2 * WCOLS], F32R) as w_lo):
            first_layer(nc, sem_ctx, s_spare, t, ident, w_hi, w_lo, attn, scratch)
            attention(nc, sem_ctx, s_spare, t, ident, w_hi, w_lo, attn, scratch)
        last_layer(nc, sem_ctx, s_spare, t, ident, attn, scratch, out)


def hadamard(np, n):
    h = np.ones((1, 1), np.float32)
    while len(h) < n:
        h = np.block([[h, h], [h, -h]])
    return h


def chunked(np, w):
    n, k = w.shape
    return np.ascontiguousarray(w.reshape(n, k // 128, 128).transpose(2, 1, 0).reshape(128, -1))


def kernel(x, itok_B_1_14, itok_Bx16_0_63, itok_B_207_1644, L0_cond_weight, L0_ffn_W_base, L0_ffn_b_base,
           L0_ffn_lora_A, L0_ffn_lora_B, L0_ffn_router_W, L0_ffn_router_b, L0_ffn_domain_prior, L0_ffn_active,
           L1_cond_Wq, L1_cond_Wk, L1_cond_Wv, L1_cond_Wo, L1_cond_q_norm_w, L1_cond_k_norm_w, L1_cond_k_cache,
           L1_cond_v_cache, L1_ffn_weight_q, L1_ffn_scales, L1_ffn_bias):
    import numpy as np
    import concourse.bacc as bacc
    from concourse.bass_utils import run_bass_kernel_spmd

    a = {k: np.asarray(v) for k, v in dict(locals()).items() if hasattr(v, "shape") and hasattr(v, "dtype")}
    x = a["x"]
    base = np.concatenate([a["L0_ffn_W_base"], a["L0_ffn_lora_A"].reshape(ZCOLS, DM), a["L0_ffn_router_W"]])
    adapter_w = a["L0_cond_weight"].reshape(ADAPTERS, DM, CH, 128).transpose(0, 3, 2, 1)
    wq = a["L1_cond_Wq"].reshape(HK, G * D, CH, 128).transpose(0, 3, 2, 1)
    wk = a["L1_cond_Wk"].reshape(HK, D, CH, 128).transpose(0, 3, 2, 1)
    wv = a["L1_cond_Wv"].reshape(HK, D, CH, 128).transpose(0, 3, 2, 1)
    wo = a["L1_cond_Wo"].reshape(DM, HK, G, D).transpose(1, 3, 2, 0)
    weights = np.concatenate([np.concatenate([wq, wk, wv], 3).reshape(HK, 128, CH * WP), wo.reshape(HK, 128, G * DM)], 2)
    weights = weights.reshape(HK, 128, B, WC).transpose(0, 2, 1, 3).reshape(STEPS, 128, WC)
    kv = np.concatenate([a["L1_cond_k_cache"], a["L1_cond_v_cache"]], 3).transpose(2, 0, 1, 3)
    inv_freq = np.float32(1.0) / np.float32(10000.0) ** (np.arange(0, D, 2, dtype=np.float32) / np.float32(D))
    row = lambda v: v.reshape(1, -1)
    arrays = {
        "x": x,
        "xt": x.reshape(B, S, CH, 128).transpose(0, 3, 2, 1).reshape(B, 128, CH * S),
        "adapter_w": adapter_w.reshape(ADAPTERS, 128, CH * DM),
        "adapters": row(a["itok_B_1_14"]),
        "w0": base.reshape(L0COLS, CH, 128).transpose(2, 1, 0),
        "lora_b": a["L0_ffn_lora_B"].transpose(0, 2, 1).reshape(ZCOLS, DM),
        "b_base": row(a["L0_ffn_b_base"]),
        "router_b": row(a["L0_ffn_router_b"]),
        "prior": row(a["L0_ffn_domain_prior"]),
        "active": row(a["L0_ffn_active"]),
        "seqlens": row(a["itok_B_207_1644"]),
        "block_table": a["itok_Bx16_0_63"],
        "norm_w": row(np.concatenate([a["L1_cond_q_norm_w"], a["L1_cond_k_norm_w"]])),
        "inv_freq": row(inv_freq),
        "weights": weights,
        "kv": kv,
        "hadamard": chunked(np, hadamard(np, DM)),
        "w8": chunked(np, a["L1_ffn_weight_q"]),
        "scales": row(a["L1_ffn_scales"]),
        "bias": row(a["L1_ffn_bias"]),
    }
    arrays = {k: np.ascontiguousarray(v) for k, v in arrays.items()}

    nc = bacc.Bacc("TRN2", target_bir_lowering=False, num_devices=1)
    t = {k: nc.dram_tensor(f"in_{k}", v.shape, mybir.dt.from_np(v.dtype), kind="ExternalInput").ap()
         for k, v in arrays.items()}
    out = nc.dram_tensor("out", (B, S, DM), F32, kind="ExternalOutput").ap()
    build(nc, t, out)
    r = run_bass_kernel_spmd(nc, [{f"in_{k}": v for k, v in arrays.items()}], core_ids=[0])
    return r.results[0]["out"]
```

```python
import concourse.bass as bass
from concourse import mybir
from contextlib import ExitStack

F32 = mybir.dt.float32
F32R = mybir.dt.float32r
I32 = mybir.dt.int32
U32 = mybir.dt.uint32
ALU = mybir.AluOpType
ACT = mybir.ActivationFunctionType
AX = mybir.AxisListType.X

B, S, DM = 8, 128, 512
CH = DM // 128
D, HQ, HK = 128, 32, 8
G = HQ // HK
ADAPTERS = 16
PAGES, PSIZE, NPP = 64, 32, 16
L = NPP * PSIZE
CT = L // 128
KT = CT + 1
KEYS = L + S
HALF = KEYS // 2
PPT = 128 // PSIZE
NE, RK = 16, 8
NACT = 4
ZCOLS = NE * RK
L0COLS = DM + ZCOLS + NE
STEPS = HK * B
WP = G * D + 2 * D
WCOLS = CH * WP + G * DM
WC = WCOLS // B
AHEAD = B + 1
CHUNKS = STEPS + B
SMALL = 2 * NE + D // 2 + 2 * D
SCALE = D ** -0.5
NORM_EPS = 1e-6
PRIOR_EPS = 1e-12
LORA_SCALE = 2.0
FP8_MAX = 448.0
MASKED = -1e30
LOWEST = -3e38
PI = 3.141592653589793
PI_IN = 3.1415925
TWO_PI_PARTS = (6.28125, 0.0019350051879882812, 2 * PI - 6.28125 - 0.0019350051879882812)
ROUND_INT = 1.5 * 2.0 ** 23
EXP_BITS = 0x7F800000
MIN_E4M3 = 2.0 ** -6
ROUND_E4M3 = 1.5 * 2.0 ** 20


class Step:

    def __init__(self, eng, value, par, spare=None):
        self.eng, self.value, self.par, self.spare = eng, value, par % 2, spare
        self.fixed = isinstance(value, int)
        self.later = {}

    def parity(self, d=0):
        return (self.par + d) % 2

    def number(self, f):
        return f(self.value) if self.fixed else self.eng.snap(f(self.value))

    def has(self, d, n):
        return not self.fixed or 0 <= self.value + d < n

    def past(self, d=0):
        if self.fixed:
            return max(self.value + d + 2, 1)
        if d not in self.later:
            self.later[d] = self.eng.snap(self.value + (d + 2))
        return self.later[d]

    def hold(self):
        self.eng.sem_inc(self.spare, 1)

    def loads(self, d=0, dmas=1):
        p = self.parity(d)
        return 16 * dmas * ((self.value + d) // 2 + 1) if self.fixed else self.eng.snap((self.value + (d - p + 2)) * (8 * dmas))


def run_steps(eng, first, loop_first, loop_end, end, body, spare=None):
    for i in range(first, loop_first):
        body(Step(eng, i, i, spare))
    with eng.Fori(loop_first // 2, loop_end // 2) as pair:
        for u in range(2):
            body(Step(eng, eng.snap(pair * 2 + u), u, spare))
    for i in range(loop_end, end):
        body(Step(eng, i, i, spare))


def names(stem, n):
    return " ".join(f"{stem}{j}" for j in range(n))


FIRST_EVENTS = {
    "pe": "c_done ct_put z_put zt_put y_put x1_done x1t_put",
    "act": "c_out ct_out expl_out zst_out x1t_hi w_hi_a",
    "dve": "logit_sum top_out logit_out alpha_mul total_out rtotal_out alpha_out zs_out x1_out x1t_lo tab_out",
    "pool": "xb_out w_lo_a x1b_out",
}
ATTENTION_EVENTS = {
    "pe": f"proj q_put kc_put kn_put wo_done {names('s_put', G)} {names('pt_put', KT)} {names('pv', KT)}",
    "act": f"qkv_out sq_out o_hi_out q_hi kc_hi kn_hi w_hi_out {names('exp', G)} {names('pt_hi_out', KT)}",
    "dve": f"ss_out q_sin_out k_parts k_sum norm o_lo_out q_lo kc_lo kn_lo rs acc {names('mx', G)} {names('nb', G)} "
           f"{names('pt_lo_out', KT)}",
    "pool": "ms rms_out q_cos_out q_sum v_hi_out v_out w_lo_out",
}
LAST_EVENTS = {
    "pe": "at_put rot qt8_put ffn",
    "act": "a_out at_hi_out abs_out scaled qt8_out",
    "dve": "at_lo_out xh_out amax_out sx_early_out sx_out rsx_out expo step_out y_out",
    "pool": "q_add q_out res_out",
}


def flat(ap):
    return ap.rearrange("o p n -> (o p) n")


def split3(nc, out, parts, first, last):
    n = len(parts)
    for j, ((a_hi, a_lo), (b_hi, b_lo)) in enumerate(parts):
        nc.tensor.matmul(out, a_hi, b_hi, start=first and j == 0, stop=False)
        nc.tensor.matmul(out, a_hi, b_lo, start=False, stop=False)
        done = nc.tensor.matmul(out, a_lo, b_hi, start=False, stop=last and j == n - 1)
    return done


def load_pages(nc, sp, t, shared, b, hk, kv, s_kv, first=0, n=NPP):
    _, pages = nc.values_load_multi_w_load_instructions(
        shared.pages[0:1, bass.ds(b * NPP + first, n)], engines=[sp.engine], min_val=0, max_val=PAGES - 1)

    def load():
        for j, page in enumerate(pages, first):
            sp.dma_start(kv[PSIZE * (j % PPT):PSIZE * (j % PPT + 1), j // PPT, :],
                         t["kv"][bass.ds(hk, 1), bass.ds(page, 1)].rearrange("a b t n -> (a b t) n")
                         ).then_inc(s_kv, 16)

    return load


def first_layer(nc, sem_ctx, s_spare, t, shared, scratch):
    x1t_dram, x1b_dram, rope_dram, mask_dram = scratch
    ident, w_hi, w_lo = shared.ident, shared.w_hi, shared.w_lo
    ctx = ExitStack()
    with ctx:
        def sb(name, shape, dt=F32):
            return ctx.enter_context(nc.sbuf_tensor(name, shape, dt))

        def bank(name):
            return ctx.enter_context(nc.psum_tensor(name, [128, 512], F32))

        def sem(name):
            return sem_ctx.enter_context(nc.semaphore(name))

        two = range(2)
        half = D // 2
        xt = [sb(f"xt{p}", [128, CH * S]) for p in two]
        xn = [sb(f"xn{p}", [128, DM]) for p in two]
        wc = [sb(f"wc{p}", [128, CH * DM]) for p in two]
        raw = [sb(f"raw_a{p}", [128, WC]) for p in two]
        w0 = sb("w0", [128, CH, L0COLS])
        lora_b = sb("lora_b", [128, DM])
        small = sb("small_rows", [128, SMALL])
        router_b, prior = small[:, 0:NE], small[:, NE:2 * NE]
        invf, norm_w = small[:, 2 * NE:2 * NE + half], small[:, 2 * NE + half:SMALL]
        biases = sb("biases", [128, 2 * DM])
        bias0, bias1 = biases[:, 0:DM], biases[:, DM:2 * DM]
        ints = sb("ints", [128, NACT + B], I32)
        ct = [sb(f"ct{p}", [128, CH * S]) for p in two]
        x1 = [sb(f"x1{p}", [128, DM]) for p in two]
        x1b = [sb("x1b0", [128, DM]), shared.x1b_odd]
        x1t = [sb("x1t0", [128, 2 * CH * S], F32R), shared.x1t_odd]
        rope = [sb(f"rope_a{p}", [128, 4 * D]) for p in two]
        mask = [sb(f"mask_a{p}", [128, KEYS]) for p in two]
        logit = sb("logit", [128, NE])
        top = sb("top", [128, 1])
        ntop = sb("ntop", [128, 1])
        expl = sb("expl", [128, NE])
        alpha = sb("alpha", [128, NE])
        total = sb("total", [128, 1])
        rtotal = sb("rtotal", [128, 1])
        zs = sb("zs", [128, ZCOLS])
        zst = sb("zst", [128, S])
        act_f = sb("act_f", [128, NACT])
        expert = sb("expert", [128, NE])
        times = sb("times", [128, NE])
        unused = sb("unused", [128, NE])
        lprior = sb("lprior", [128, NE])
        lbias = sb("lbias", [128, NE])
        eps_col = sb("eps_col", [128, 1])
        seq_f = sb("seq_f", [128, B])
        tok = sb("tok", [128, 1])
        pos = sb("pos", [128, B])
        spare = shared.attn
        key_no = spare[:, 0:L]
        factor = spare[:, L:L + 8 * half].rearrange("p (k j m n) -> p k j m n", k=2, j=2, m=2)
        angle, turns, cos, sin = (spare[:, n:n + B * half].rearrange("p (b n) -> p b n", b=B)
                                  for n in range(L + 8 * half, L + (8 + 4 * B) * half, B * half))
        c_sb = [spare[:, n:n + DM] for n in (B * DM - 2 * DM, B * DM - DM)]

        c_bank = bank("c_bank")
        ct_bank = bank("ct_bank")
        z_bank = [bank(f"z_bank{p}") for p in two]
        y_bank = [bank(f"y_bank{p}") for p in two]
        zt_bank = bank("zt_bank")
        xt_bank = bank("xt_bank")

        ev = shared.ev
        s_xt = [sem(f"s_xt{p}") for p in two]
        s_xn = [sem(f"s_xn{p}") for p in two]
        s_wc = [sem(f"s_wc{p}") for p in two]
        s_raw = [sem(f"s_raw_a{p}") for p in two]
        s_st = shared.s_st
        s_tab = [sem(f"s_tab{p}") for p in two]
        s_w0, s_rows, s_wide, s_consts = sem("s_w0"), sem("s_rows"), sem("s_wide"), sem("s_consts")
        s_pages = sem("s_pages")
        s_v, s_prior, s_sin, s_router = sem("s_v"), sem("s_prior"), sem("s_sin"), sem("s_router")

        block = ctx.enter_context(nc.Block())
        END = B + 2

        @block.sync
        def _(sp):
            def body(st):
                p, q = st.parity(), st.parity(-1)
                if st.has(1, B):
                    i = st.number(lambda v: v + 1)
                    adapter = sp.value_load(t["adapters"][0:1, bass.ds(i, 1)], min_val=0, max_val=ADAPTERS - 1)
                    sp.wait_ge(ev["c_done"], st.past(-1))
                    st.hold()
                    sp.dma_start(xt[q][:, :], flat(t["xt"][bass.ds(i, 1)])).then_inc(s_xt[q], 16)
                    sp.dma_start(wc[q][:, :], flat(t["adapter_w"][bass.ds(adapter, 1)])).then_inc(s_wc[q], 16)
                if st.fixed and st.value == -1:
                    sp.dma_start(shared.pages[:, :], t["block_table"]).then_inc(s_pages, 16)
                    sp.dma_start(small[:, :], t["small_rows"].partition_broadcast(128)).then_inc(s_rows, 16)
                    sp.dma_start(ints[:, :], t["ints"].partition_broadcast(128)).then_inc(s_rows, 16)
                if st.has(1, AHEAD):
                    i = st.number(lambda v: v + 1)
                    sp.wait_ge(ev["w_lo_a"], st.past(-1))
                    st.hold()
                    sp.dma_start(raw[q][:, :], flat(t["weights"][bass.ds(i, 1)])).then_inc(s_raw[q], 16)
                if st.has(0, B):
                    sp.wait_ge(ev["x1_out"], st.past(-2))
                    st.hold()
                    sp.dma_start(xn[p][:, :], flat(t["x"][bass.ds(st.value, 1)])).then_inc(s_xn[p], 16)
                if st.fixed and st.value == 0:
                    for c in range(CH):
                        sp.dma_start(w0[:, c, :], t["w0"][:, c, :]).then_inc(s_w0, 16)
                    sp.dma_start(lora_b[:, :], t["lora_b"]).then_inc(s_w0, 16)
                    sp.dma_start(biases[:, :], t["biases"].partition_broadcast(128)).then_inc(s_wide, 16)
                    sp.dma_start(shared.scales[:, :], t["scales"].partition_broadcast(128)).then_inc(s_wide, 16)
                if st.has(-2, B):
                    j = st.number(lambda v: v - 2)
                    sp.wait_ge(ev["tab_out"], st.past(-2))
                    st.hold()
                    sp.dma_start(flat(rope_dram[bass.ds(j, 1)]), rope[p][:, :]).then_inc(s_tab[p], 16)
                    sp.dma_start(flat(mask_dram[bass.ds(j, 1)]), mask[p][0:1, :]).then_inc(s_tab[p], 16)
                if st.has(-3, B):
                    j = st.number(lambda v: v - 3)
                    sp.wait_ge(ev["x1b_out"], st.past(-3))
                    sp.wait_ge(ev["x1t_hi"], st.past(-3))
                    sp.wait_ge(ev["x1t_lo"], st.past(-3))
                    st.hold()
                    sp.dma_start(flat(x1b_dram[bass.ds(j, 1)]), x1b[q][:, :]).then_inc(s_st[q], 16)
                    sp.dma_start(flat(x1t_dram[bass.ds(j, 1)]), x1t[q][:, :].bitcast(F32)).then_inc(s_st[q], 16)
                if st.fixed and st.value == 0:
                    sp.wait_ge(s_pages, 16)
                if st.has(0, B):
                    u, quarter = divmod(st.value, B // 2) if st.fixed else (1, p)
                    load_pages(nc, sp, t, shared, u, 0, shared.kv[u], shared.s_kv[u], NPP // 4 * quarter, NPP // 4)()
                if st.fixed and st.value == B - 1:
                    sp.wait_ge(s_tab[0], 32)
                    sp.wait_ge(s_st[0], 32)
                    sp.dma_start(shared.rope[0][:, :], flat(rope_dram[0:1])).then_inc(shared.s_rope[0], 16)
                    sp.dma_start(shared.x1t[0][:, :].bitcast(F32), flat(x1t_dram[0:1])).then_inc(shared.s_x1t[0], 16)
                    sp.dma_start(shared.mask[0][:, :], flat(mask_dram[0:1]).partition_broadcast(128)).then_inc(shared.s_mask[0], 16)

            run_steps(sp, -1, B // 2, B // 2 + 2, END + 1, body, s_spare)
            for p in two:
                sp.wait_ge(s_tab[p], 16 * B)
            sp.wait_ge(s_st[0], 16 * B)

        @block.tensor
        def _(pe):
            for s in shared.by_engine["pe"]:
                pe.sem_inc(s, 1)
            pe.wait_ge(s_consts, 2)

            def body(st):
                p, q = st.parity(), st.parity(-1)
                if st.has(-1, B):
                    pe.wait_ge(ev["c_out"], st.past(-1))
                    pe.wait_ge(ev["ct_out"], st.past(-2))
                    for c in range(CH):
                        last = nc.tensor.transpose(ct_bank[:, c * 128:(c + 1) * 128],
                                                   c_sb[q][:, c * 128:(c + 1) * 128], ident[:, :])
                    last.then_inc(ev["ct_put"], 1)
                if st.has(-2, B):
                    pe.wait_ge(ev["zs_out"], st.past(-2))
                    pe.wait_ge(ev["zst_out"], st.past(-3))
                    nc.tensor.transpose(zt_bank[:, 0:S], zs[:, :], ident[:, :]).then_inc(ev["zt_put"], 1)
                if st.has(0, B):
                    pe.wait_ge(s_xt[st.parity()], st.loads())
                    pe.wait_ge(s_wc[st.parity()], st.loads())
                    pe.wait_ge(ev["c_out"], st.past(-1))
                    for c in range(CH):
                        last = nc.tensor.matmul(c_bank[:, :], xt[p][:, c * S:(c + 1) * S],
                                                wc[p][:, c * DM:(c + 1) * DM], start=c == 0, stop=c == CH - 1)
                    last.then_inc(ev["c_done"], 1)
                if st.has(-2, B):
                    pe.wait_ge(ev["zst_out"], st.past(-2))
                    nc.tensor.matmul(y_bank[p][:, :], zst[:, :], lora_b[:, :], start=False, stop=True).then_inc(ev["x1_done"], 1)
                if st.has(-1, B):
                    if st.fixed and st.value == 1:
                        pe.wait_ge(s_w0, 16 * (CH + 1))
                    pe.wait_ge(ev["ct_out"], st.past(-1))
                    pe.wait_ge(ev["zs_out"], st.past(-3))
                    pe.wait_ge(ev["x1_out"], st.past(-3))
                    for c in range(CH):
                        last = nc.tensor.matmul(z_bank[q][:, 0:ZCOLS + NE], ct[q][:, c * 128:(c + 1) * 128],
                                                w0[:, c, DM:L0COLS], start=c == 0, stop=c == CH - 1)
                    last.then_inc(ev["z_put"], 1)
                    for c in range(CH):
                        last = nc.tensor.matmul(y_bank[q][:, :], ct[q][:, c * 128:(c + 1) * 128],
                                                w0[:, c, 0:DM], start=c == 0, stop=False)
                    last.then_inc(ev["y_put"], 1)
                if st.has(-2, B):
                    pe.wait_ge(ev["x1_out"], st.past(-2))
                    pe.wait_ge(ev["x1t_lo"], st.past(-3))
                    for c in range(CH):
                        last = nc.tensor.transpose(xt_bank[:, c * 128:(c + 1) * 128],
                                                   x1[p][:, c * 128:(c + 1) * 128], ident[:, :])
                    last.then_inc(ev["x1t_put"], 1)

            run_steps(pe, 0, 2, B, END, body)

        @block.scalar
        def _(act):
            for s in shared.by_engine["act"]:
                act.sem_inc(s, 1)
            act.wait_ge(s_rows, 32)
            act.wait_ge(s_prior, 1)
            nc.scalar.activation(lprior[:, :], prior, ACT.Ln, bias=eps_col[:, :]).then_inc(s_router, 1)

            def body(st):
                p, q = st.parity(), st.parity(-1)
                if st.has(-1, B):
                    act.wait_ge(ev["ct_put"], st.past(-1))
                    act.wait_ge(ev["y_put"], st.past(-3))
                    nc.scalar.copy(ct[q][:, :], ct_bank[:, :]).then_inc(ev["ct_out"], 1)
                if st.has(-2, B):
                    act.wait_ge(ev["zt_put"], st.past(-2))
                    act.wait_ge(ev["x1_done"], st.past(-3))
                    nc.scalar.copy(zst[:, :], zt_bank[:, 0:S]).then_inc(ev["zst_out"], 1)
                if st.has(0, B):
                    act.wait_ge(ev["c_done"], st.past())
                    act.wait_ge(ev["ct_put"], st.past(-2))
                    nc.scalar.copy(c_sb[p][:, :], c_bank[:, :]).then_inc(ev["c_out"], 1)
                if st.fixed and st.value == 0:
                    act.wait_ge(s_sin, 1)
                    nc.scalar.activation(sin[:, :, :], angle[:, :, :], ACT.Sin).then_inc(s_sin, 1)
                    act.wait_ge(s_sin, 3)
                    nc.scalar.activation(cos[:, :, :], turns[:, :, :], ACT.Sin).then_inc(s_sin, 1)
                if st.has(0, AHEAD):
                    act.wait_ge(s_raw[st.parity()], st.loads())
                    nc.scalar.copy(w_hi[:, bass.ds(st.number(lambda v: v * WC), WC)], raw[p][:, :]).then_inc(ev["w_hi_a"], 1)
                if st.has(-1, B):
                    act.wait_ge(ev["logit_out"], st.past(-1))
                    act.wait_ge(ev["zs_out"], st.past(-2))
                    nc.scalar.activation(expl[:, :], logit[:, :], ACT.Exp, bias=ntop[:, :]).then_inc(ev["expl_out"], 1)
                if st.has(-2, B):
                    act.wait_ge(ev["x1t_put"], st.past(-2))
                    if not st.fixed or st.value >= 4:
                        act.wait_ge(s_st[st.parity(-4)], st.loads(-4, 2))
                    nc.scalar.copy(x1t[p][:, 0:CH * S], xt_bank[:, :]).then_inc(ev["x1t_hi"], 1)

            run_steps(act, 0, 4, B, END, body)

        @block.gpsimd
        def _(pool):
            for s in shared.by_engine["pool"]:
                pool.sem_inc(s, 1)
            nc.gpsimd.memset(ident[:, :], 0.0).then_inc(s_consts, 1)
            nc.gpsimd.memset(eps_col[:, :], PRIOR_EPS).then_inc(s_prior, 1)
            pool.wait_ge(s_consts, 1)
            nc.gpsimd.affine_select(out=ident[:, :], in_=ident[:, :], compare_op=ALU.not_equal, fill=1.0,
                                    base=0, pattern=[[-1, 128]], channel_multiplier=1).then_inc(s_consts, 1)
            nc.gpsimd.iota(expert[:, :], pattern=[[1, NE]], base=0, channel_multiplier=0,
                           allow_small_or_imprecise_dtypes=True)
            nc.gpsimd.iota(tok[:, :], pattern=[[1, 1]], base=0, channel_multiplier=1,
                           allow_small_or_imprecise_dtypes=True)
            nc.gpsimd.iota(key_no, pattern=[[1, L]], base=0, channel_multiplier=0,
                           allow_small_or_imprecise_dtypes=True)
            for p in two:
                last = nc.gpsimd.memset(mask[p][:, L:KEYS], 0.0)
            last.then_inc(s_consts, 1)
            pool.wait_ge(s_wide, 32)

            def body(st):
                p = st.parity()
                if st.has(0, B):
                    pool.wait_ge(s_xn[st.parity()], st.loads())
                    nc.gpsimd.tensor_tensor(xn[p][:, :], xn[p][:, :], bias0, ALU.add).then_inc(ev["xb_out"], 1)
                if st.has(0, AHEAD):
                    pool.wait_ge(ev["w_hi_a"], st.past())
                    at = bass.ds(st.number(lambda v: v * WC), WC)
                    nc.gpsimd.tensor_tensor(w_lo[:, at], raw[p][:, :], w_hi[:, at].bitcast(F32),
                                            ALU.subtract).then_inc(ev["w_lo_a"], 1)
                if st.fixed and st.value == B + 1:
                    pool.wait_ge(ev["tab_out"], st.past(-2))
                    nc.gpsimd.memset(shared.attn[:, :], 0.0)
                if st.has(-2, B):
                    pool.wait_ge(ev["x1_out"], st.past(-2))
                    if not st.fixed or st.value >= 4:
                        pool.wait_ge(s_st[st.parity(-4)], st.loads(-4, 2))
                    nc.gpsimd.tensor_tensor(x1b[p][:, :], x1[p][:, :], bias1, ALU.add).then_inc(ev["x1b_out"], 1)

            run_steps(pool, 0, 4, B, END, body)

        @block.vector
        def _(dve):
            for s in shared.by_engine["dve"]:
                dve.sem_inc(s, 1)
            count = [0]

            def chain(ins):
                count[0] += 1
                ins.then_inc(s_v, 1)
                dve.wait_ge(s_v, count[0])

            dve.wait_ge(s_consts, 3)
            dve.wait_ge(s_rows, 32)
            nc.vector.tensor_copy(act_f[:, :], ints[:, 0:NACT])
            nc.vector.tensor_copy(seq_f[:, :], ints[:, NACT:NACT + B])
            chain(nc.vector.memset(times[:, :], 0.0))
            for a in range(NACT):
                chain(nc.vector.scalar_tensor_tensor(out=times[:, :], in0=expert[:, :], scalar=act_f[:, a:a + 1],
                                                     in1=times[:, :], op0=ALU.is_equal, op1=ALU.add))
            chain(nc.vector.tensor_scalar(unused[:, :], times[:, :], 0.0, MASKED, ALU.is_equal, ALU.mult))
            dve.wait_ge(s_router, 1)
            chain(nc.vector.tensor_tensor(lbias[:, :], lprior[:, :], router_b, ALU.add))
            chain(nc.vector.tensor_tensor(lbias[:, :], lbias[:, :], unused[:, :], ALU.add))

            def angles():
                chain(nc.vector.tensor_scalar(pos[:, :], seq_f[:, :], tok[:, :], None, ALU.add))
                pos_b = pos[:, :].unsqueeze(2).to_broadcast([128, B, half])
                invf_b = invf.unsqueeze(1).to_broadcast([128, B, half])
                chain(nc.vector.tensor_tensor(angle[:, :, :], pos_b, invf_b, ALU.mult))
                chain(nc.vector.tensor_scalar(turns[:, :, :], angle[:, :, :], 0.5 / PI, 0.25, ALU.mult, ALU.add))
                chain(nc.vector.tensor_scalar(turns[:, :, :], turns[:, :, :], ROUND_INT, -ROUND_INT, ALU.add, ALU.add))
                chain(nc.vector.scalar_tensor_tensor(out=cos[:, :, :], in0=turns[:, :, :], scalar=-TWO_PI_PARTS[0],
                                                     in1=angle[:, :, :], op0=ALU.mult, op1=ALU.add))
                for part in TWO_PI_PARTS[1:]:
                    chain(nc.vector.scalar_tensor_tensor(out=cos[:, :, :], in0=turns[:, :, :], scalar=-part,
                                                         in1=cos[:, :, :], op0=ALU.mult, op1=ALU.add))
                chain(nc.vector.tensor_scalar(turns[:, :, :], angle[:, :, :], 0.5 / PI, ROUND_INT, ALU.mult, ALU.add))
                chain(nc.vector.tensor_scalar(turns[:, :, :], turns[:, :, :], -ROUND_INT, None, ALU.add))
                for part in TWO_PI_PARTS:
                    chain(nc.vector.scalar_tensor_tensor(out=angle[:, :, :], in0=turns[:, :, :], scalar=-part,
                                                         in1=angle[:, :, :], op0=ALU.mult, op1=ALU.add))
                nc.vector.tensor_scalar(angle[:, :, :], angle[:, :, :], PI_IN, -PI_IN, ALU.min, ALU.max).then_inc(s_sin, 1)
                chain(nc.vector.tensor_scalar(turns[:, :, :], cos[:, :, :], PI / 2, PI_IN, ALU.add, ALU.min))
                nc.vector.tensor_scalar(turns[:, :, :], turns[:, :, :], -PI_IN, None, ALU.max).then_inc(s_sin, 1)
                for k, scale in ((0, SCALE), (1, 1.0)):
                    w1, w2 = (norm_w[:, k * D + lo:k * D + lo + half] for lo in (0, half))
                    for j, (w, sign) in enumerate(((w1, 1.0), (w2, 1.0), (w2, -1.0), (w1, 1.0))):
                        last = nc.vector.tensor_scalar(factor[:, k, j // 2, j % 2, :], w, sign * scale, None, ALU.mult)
                chain(last)

            angles()

            def body(st):
                p, q = st.parity(), st.parity(-1)
                if st.has(-2, B):
                    dve.wait_ge(ev["x1_done"], st.past(-2))
                    dve.wait_ge(ev["xb_out"], st.past(-2))
                    dve.wait_ge(ev["x1t_put"], st.past(-4))
                    dve.wait_ge(ev["x1b_out"], st.past(-4))
                    nc.vector.tensor_tensor(x1[p][:, :], y_bank[p][:, :], xn[p][:, :], ALU.add).then_inc(ev["x1_out"], 1)
                if st.has(-1, B):
                    dve.wait_ge(ev["z_put"], st.past(-1))
                    dve.wait_ge(ev["expl_out"], st.past(-2))
                    nc.vector.tensor_tensor(logit[:, :], z_bank[q][:, ZCOLS:ZCOLS + NE], lbias[:, :],
                                            ALU.add).then_inc(ev["logit_sum"], 1)
                    dve.wait_ge(ev["logit_sum"], st.past(-1))
                    nc.vector.reduce_max(top[:, :], logit[:, :], AX).then_inc(ev["top_out"], 1)
                    dve.wait_ge(ev["top_out"], st.past(-1))
                    nc.vector.tensor_scalar(ntop[:, :], top[:, :], -1.0, None, ALU.mult).then_inc(ev["logit_out"], 1)
                    dve.wait_ge(ev["expl_out"], st.past(-1))
                    nc.vector.tensor_tensor(alpha[:, :], expl[:, :], times[:, :], ALU.mult).then_inc(ev["alpha_mul"], 1)
                    dve.wait_ge(ev["alpha_mul"], st.past(-1))
                    nc.vector.reduce_sum(total[:, :], alpha[:, :], AX).then_inc(ev["total_out"], 1)
                    dve.wait_ge(ev["total_out"], st.past(-1))
                    nc.vector.reciprocal(rtotal[:, :], total[:, :]).then_inc(ev["rtotal_out"], 1)
                    dve.wait_ge(ev["rtotal_out"], st.past(-1))
                    nc.vector.tensor_scalar(alpha[:, :], alpha[:, :], rtotal[:, :], LORA_SCALE, ALU.mult,
                                            ALU.mult).then_inc(ev["alpha_out"], 1)
                    dve.wait_ge(ev["alpha_out"], st.past(-1))
                    dve.wait_ge(ev["zt_put"], st.past(-2))
                    nc.vector.tensor_tensor(zs[:, :].rearrange("p (e r) -> p e r", r=RK),
                                            z_bank[q][:, 0:ZCOLS].rearrange("p (e r) -> p e r", r=RK),
                                            alpha[:, :].unsqueeze(2).to_broadcast([128, NE, RK]),
                                            ALU.mult).then_inc(ev["zs_out"], 1)
                    if st.fixed and st.value == 1:
                        dve.wait_ge(s_sin, 4)
                    if not st.fixed or st.value >= 3:
                        dve.wait_ge(s_tab[st.parity(-3)], st.loads(-3, 2))
                    b = st.number(lambda v: v - 1)
                    for j, wave in enumerate((cos, sin)):
                        table = rope[q][:, :].rearrange("p (k j m n) -> p k j m n", k=2, j=2, m=2)[:, :, j]
                        for k in range(2):
                            nc.vector.tensor_tensor(table[:, k], factor[:, k, j],
                                                    wave[:, bass.ds(b, 1), :].to_broadcast([128, 2, half]), ALU.mult)
                    nc.vector.tensor_scalar(mask[q][:, 0:L], key_no, seq_f[:, bass.ds(b, 1)], MASKED,
                                            ALU.is_ge, ALU.mult).then_inc(ev["tab_out"], 1)
                if st.has(-2, B):
                    dve.wait_ge(ev["x1t_hi"], st.past(-2))
                    nc.vector.tensor_tensor(x1t[p][:, CH * S:2 * CH * S], xt_bank[:, :],
                                            x1t[p][:, 0:CH * S].bitcast(F32), ALU.subtract).then_inc(ev["x1t_lo"], 1)

            run_steps(dve, 0, 4, B, END, body)


def attention(nc, sem_ctx, s_spare, t, shared, scratch):
    x1t_dram, _, rope_dram, mask_dram = scratch
    ident, attn, w_hi, w_lo = shared.ident, shared.attn, shared.w_hi, shared.w_lo
    kv, x1t, rope, mask = shared.kv, shared.x1t, shared.rope, shared.mask
    s_kv, s_x1t, s_rope, s_mask = shared.s_kv, shared.s_x1t, shared.s_rope, shared.s_mask
    ctx = ExitStack()
    with ctx:
        def sb(name, shape, dt=F32):
            return ctx.enter_context(nc.sbuf_tensor(name, shape, dt))

        def sem(name):
            return sem_ctx.enter_context(nc.semaphore(name))

        two = range(2)
        raw = [sb(f"raw{p}", [128, WC]) for p in two]
        qkv = sb("qkv", [128, WP])
        sq = sb("sq", [128, (G + 1) * D])
        ssum = sb("ssum", [128, G + 1])
        half_neg = sb("half_neg", [128, G + 1])
        rms = [sb(f"rms{p}", [128, G + 1]) for p in two]
        q_cos, q_sin, q_rot = (sb(n, [128, G * D]) for n in ("q_cos", "q_sin", "q_rot"))
        k_cos, k_sin, k_rot = (sb(n, [128, D]) for n in ("k_cos", "k_sin", "k_rot"))
        qt_hi, qt_lo = (sb(n, [128, G * S], F32R) for n in ("qt_hi", "qt_lo"))
        kt_hi, kt_lo = (sb(n, [128, KEYS], F32R) for n in ("kt_hi", "kt_lo"))
        v_hi = [sb(f"v_hi{p}", [128, KT, D], F32R) for p in two]
        v_lo = [sb(f"v_lo{p}", [128, KT, D], F32R) for p in two]
        score = [sb(f"score{p}", [128, KEYS]) for p in two]
        top = sb("top_score", [128, G])
        nbias = sb("nbias", [128, G])
        prob = [sb(f"prob{p}", [128, G, KEYS]) for p in two]
        psum_row = [sb(f"row_sum{p}", [128, G]) for p in two]
        rsum = sb("rsum", [128, G])
        pt_hi = [sb(f"pt_hi{p}", [128, G * S], F32R) for p in two]
        pt_lo = [sb(f"pt_lo{p}", [128, G * S], F32R) for p in two]
        o_hi, o_lo = (sb(n, [128, G * S], F32R) for n in ("o_hi", "o_lo"))

        slot = [ctx.enter_context(nc.psum_tensor(f"slot{p}", [128, 1024], F32)) for p in two]
        ring = [ctx.enter_context(nc.psum_tensor(f"ring{p}", [128, 512], F32)) for p in two]
        o_bank = ctx.enter_context(nc.psum_tensor("o_bank", [128, 512], F32))
        wo_bank = ctx.enter_context(nc.psum_tensor("wo_bank", [128, 512], F32))

        heads, tiles = range(G), range(KT)
        names = lambda stem, over: " ".join(f"{stem}{j}" for j in over)
        ev = shared.ev
        s_raw = [sem(f"s_raw{p}") for p in two]
        s_half = sem("s_half")

        block = ctx.enter_context(nc.Block())
        FIRST, LOOP0, LOOP1, END = -1, 2, STEPS - 2, STEPS + 2

        @block.sync
        def _(sp):
            def body(st):
                p, q = st.parity(), st.parity(1)
                if st.fixed and st.value == FIRST:
                    sp.dma_start(x1t[1][:, :].bitcast(F32), flat(x1t_dram[1:2])).then_inc(s_x1t[1], 16)
                    sp.dma_start(rope[1][:, :], flat(rope_dram[1:2])).then_inc(s_rope[1], 16)
                if st.fixed and st.value == 0:
                    sp.wait_ge(shared.s_st[1], 16 * B)
                if st.has(0, STEPS) and st.has(2, STEPS):
                    b = st.number(lambda v: (v + 2) & (B - 1))
                    sp.wait_ge(ev["proj"], st.past())
                    st.hold()
                    sp.dma_start(x1t[p][:, :].bitcast(F32), flat(x1t_dram[bass.ds(b, 1)])).then_inc(s_x1t[p], 16)
                if st.has(1, CHUNKS - AHEAD):
                    chunk = st.number(lambda v: v + 1 + AHEAD)
                    sp.wait_ge(ev["w_lo_out"], st.past(-1))
                    st.hold()
                    sp.dma_start(raw[q][:, :], flat(t["weights"][bass.ds(chunk, 1)])).then_inc(s_raw[q], 16)
                if st.has(0, STEPS) and st.has(2, STEPS):
                    sp.wait_ge(ev["k_parts"], st.past())
                    sp.wait_ge(ev["q_sin_out"], st.past())
                    sp.wait_ge(ev["q_cos_out"], st.past())
                    st.hold()
                    sp.dma_start(rope[p][:, :], flat(rope_dram[bass.ds(b, 1)])).then_inc(s_rope[p], 16)
                if st.has(0, STEPS) and st.has(1, STEPS):
                    b = st.number(lambda v: (v + 1) & (B - 1))
                    sp.wait_ge(ev["mx3"], st.past(-1))
                    st.hold()
                    sp.dma_start(mask[q][:, :], flat(mask_dram[bass.ds(b, 1)]).partition_broadcast(128)).then_inc(s_mask[q], 16)
                if st.has(0, STEPS) and st.has(2, STEPS):
                    b = st.number(lambda v: (v + 2) & (B - 1))
                    hk = st.number(lambda v: (v + 2) >> 3 & (HK - 1))
                    load = load_pages(nc, sp, t, shared, b, hk, kv[p], s_kv[p])
                    sp.wait_ge(ev["kc_put"], st.past())
                    sp.wait_ge(ev["v_out"], st.past())
                    st.hold()
                    load()

            run_steps(sp, FIRST, LOOP0, LOOP1, END, body, s_spare)

        @block.tensor
        def _(pe):

            def body(st):
                i0, i1 = st.parity(), st.parity(1)
                def key_transpose():
                    pe.wait_ge(ev["k_sum"], st.past())
                    pe.wait_ge(ev["q_lo"], st.past())
                    nc.tensor.transpose(ring[1][:, 0:S], k_rot[:, :], ident[:, :]).then_inc(ev["kn_put"], 1)

                def projections(d):
                    at = st.number(lambda v: ((v + d) >> 3 & 1) * WCOLS)
                    u = st.parity(d)
                    pe.wait_ge(s_x1t[u], st.loads(d))
                    if not (st.fixed and st.value < 0):
                        pe.wait_ge(ev["w_lo_out"], st.past(-1))
                    pe.wait_ge(ev["mx2"], st.past(-1))
                    xh = [x1t[u][:, c * S:(c + 1) * S] for c in range(CH)]
                    xl = [x1t[u][:, (CH + c) * S:(CH + c + 1) * S] for c in range(CH)]
                    wh, wl = w_hi[:, bass.ds(at, CH * WP)], w_lo[:, bass.ds(at, CH * WP)]
                    for lo, hi in ((0, G * D), (G * D, WP)):
                        if lo and st.has(0, STEPS):
                            key_transpose()
                        last = split3(nc, slot[1 - u][:, lo:hi],
                                      [((xh[c], xl[c]), (wh[:, c * WP + lo:c * WP + hi], wl[:, c * WP + lo:c * WP + hi]))
                                       for c in range(CH)], True, True)
                    last.then_inc(ev["proj"], 1)

                if st.has(1, STEPS) and not (st.fixed and st.value == 0):
                    projections(1)
                elif st.has(0, STEPS):
                    key_transpose()
                if st.fixed and st.value == FIRST:
                    projections(2)

                def values_transpose(kt):
                    if kt == 0:
                        pe.wait_ge(ev["norm"], st.past(-1))
                    if kt >= 2:
                        pe.wait_ge(ev[f"pt_lo_out{kt - 2}"], st.past(-1))
                    elif st.has(0, STEPS):
                        pe.wait_ge(ev["kn_lo" if kt else "kc_lo"], st.past())
                    else:
                        pe.wait_ge(ev[f"pt_lo_out{4 - kt}"], st.past(-2))
                    bank = ring[kt % 2]
                    for h in heads:
                        last = nc.tensor.transpose(bank[:, h * S:(h + 1) * S],
                                                   prob[i1][:, h, kt * 128:(kt + 1) * 128], ident[:, :])
                    last.then_inc(ev[f"pt_put{kt}"], 1)

                def values_product(kt):
                    pe.wait_ge(ev[f"pt_lo_out{kt}"], st.past(-1))
                    if kt == 0:
                        pe.wait_ge(ev["v_out"], st.past(-1))
                        pe.wait_ge(ev["o_lo_out"], st.past(-2))
                    u = st.parity(-1 + kt)
                    split3(nc, o_bank[:, :], [((v_hi[i1][:, kt, :], v_lo[i1][:, kt, :]), (pt_hi[u][:, :], pt_lo[u][:, :]))],
                           kt == 0, kt == KT - 1).then_inc(ev[f"pv{kt}"], 1)

                def scores(h):
                    if h == 0:
                        pe.wait_ge(ev["q_lo"], st.past())
                        pe.wait_ge(ev["kc_lo"], st.past())
                        pe.wait_ge(ev["kn_lo"], st.past())
                    if h == 1:
                        if st.has(1, STEPS):
                            pe.wait_ge(ev["sq_out"], st.past(1))
                        else:
                            pe.wait_ge(ev["mx2"], st.past(-1))
                    else:
                        pe.wait_ge(ev["mx3" if h == 0 else f"mx{h - 2}"], st.past(-1 if h == 0 else 0))
                    halves = slot[st.parity(1 + h)][:, :].rearrange("p (b n) -> p b n", b=2)
                    qh, ql = qt_hi[:, h * S:(h + 1) * S], qt_lo[:, h * S:(h + 1) * S]
                    for a, k, first, final in ((qh, kt_hi, True, False), (qh, kt_lo, False, False), (ql, kt_hi, False, True)):
                        for b in two:
                            last = nc.tensor.matmul(halves[:, b, 0:HALF], a, k[:, b * HALF:(b + 1) * HALF], start=first, stop=final)
                    last.then_inc(ev[f"s_put{h}"], 1)

                ending = not st.has(1, STEPS)
                if st.has(-1, STEPS) and not ending:
                    values_transpose(0)
                if st.has(-2, STEPS):
                    at = st.number(lambda v: ((v - 2) >> 3 & 1) * WCOLS + CH * WP)
                    pe.wait_ge(ev["o_lo_out"], st.past(-2))
                    pe.wait_ge(ev["acc"], st.past(-3))
                    wh, wl = w_hi[:, bass.ds(at, G * DM)], w_lo[:, bass.ds(at, G * DM)]
                    split3(nc, wo_bank[:, :],
                           [((o_hi[:, h * S:(h + 1) * S], o_lo[:, h * S:(h + 1) * S]),
                             (wh[:, h * DM:(h + 1) * DM], wl[:, h * DM:(h + 1) * DM])) for h in heads],
                           True, True).then_inc(ev["wo_done"], 1)
                if st.has(-1, STEPS) and ending:
                    values_transpose(0)
                for u in range(G - 1):
                    if st.has(-1, STEPS):
                        values_transpose(u + 1)
                    if st.has(0, STEPS):
                        scores(u)
                    if st.has(-1, STEPS):
                        values_product(u)
                if st.has(-1, STEPS):
                    values_transpose(KT - 1)
                if st.has(0, STEPS):
                    scores(G - 1)
                if st.has(1, STEPS):
                    pe.wait_ge(ev["q_sum"], st.past(1))
                    pe.wait_ge(ev["pt_lo_out3"], st.past(-1))
                    for h in heads:
                        last = nc.tensor.transpose(ring[1][:, h * S:(h + 1) * S], q_rot[:, h * D:(h + 1) * D], ident[:, :])
                    last.then_inc(ev["q_put"], 1)
                if st.has(-1, STEPS):
                    values_product(KT - 2)
                if st.has(1, STEPS):
                    pe.wait_ge(s_kv[st.parity(1)], st.loads(1, NPP))
                    pe.wait_ge(ev["pt_lo_out4"], st.past(-1))
                    for c in range(CT):
                        last = nc.tensor.transpose(ring[0][:, c * 128:(c + 1) * 128], kv[i1][:, c, 0:D], ident[:, :])
                    last.then_inc(ev["kc_put"], 1)
                if st.has(-1, STEPS):
                    values_product(KT - 1)

            run_steps(pe, FIRST, LOOP0, LOOP1, END, body)

        @block.scalar
        def _(act):

            def body(st):
                i0, i1 = st.parity(), st.parity(1)

                def probs_hi(kt):
                    u = st.parity(-1 + kt)
                    act.wait_ge(ev[f"pt_put{kt}"], st.past(-1))
                    act.wait_ge(ev[f"pv{kt - 2}" if kt >= 2 else f"pv{kt + 3}"], st.past(-1 if kt >= 2 else -2))
                    nc.scalar.copy(pt_hi[u][:, :], ring[kt % 2][:, :]).then_inc(ev[f"pt_hi_out{kt}"], 1)

                if st.has(-2, STEPS):
                    act.wait_ge(ev["pv4"], st.past(-2))
                    act.wait_ge(ev["wo_done"], st.past(-3))
                    nc.scalar.copy(o_hi[:, :], o_bank[:, :]).then_inc(ev["o_hi_out"], 1)
                if st.has(0, STEPS):
                    act.wait_ge(ev["kc_put"], st.past())
                    nc.scalar.copy(kt_hi[:, 0:L], ring[0][:, :]).then_inc(ev["kc_hi"], 1)
                if st.has(0, CHUNKS - AHEAD):
                    act.wait_ge(s_raw[st.parity()], st.loads())
                    act.wait_ge(ev["proj"], st.past())
                    act.wait_ge(ev["wo_done"], st.past(-3))
                    at = st.number(lambda v: ((v + AHEAD) >> 3 & 1) * WCOLS + ((v + AHEAD) & (B - 1)) * WC)
                    nc.scalar.copy(w_hi[:, bass.ds(at, WC)], raw[i0][:, :]).then_inc(ev["w_hi_out"], 1)
                elif st.fixed and 0 <= st.value < STEPS:
                    act.sem_inc(ev["w_hi_out"], 1)
                if st.has(0, STEPS):
                    act.wait_ge(ev["kn_put"], st.past())
                    nc.scalar.copy(kt_hi[:, L:KEYS], ring[1][:, 0:S]).then_inc(ev["kn_hi"], 1)
                if st.has(1, STEPS):
                    act.wait_ge(ev["proj"], st.past(1))
                    act.wait_ge(ev["q_cos_out"], st.past())
                    act.wait_ge(ev["q_sin_out"], st.past())
                    act.wait_ge(ev["k_parts"], st.past())
                    act.wait_ge(ev["v_out"], st.past())
                    nc.scalar.copy(qkv[:, :], slot[i0][:, 0:WP]).then_inc(ev["qkv_out"], 1)
                    act.wait_ge(ev["ss_out"], st.past())
                    nc.scalar.activation(sq[:, :], slot[i0][:, 0:(G + 1) * D], ACT.Square).then_inc(ev["sq_out"], 1)
                if st.has(-1, STEPS):
                    probs_hi(0)

                def exps(h):
                    act.wait_ge(ev[f"nb{h}"], st.past())
                    if h == 0:
                        act.wait_ge(ev["pt_put4"], st.past(-2))
                        act.wait_ge(ev["rs"], st.past(-2))
                    nc.scalar.activation(prob[i0][:, h, :], score[h % 2][:, :], ACT.Exp, bias=nbias[:, h:h + 1],
                                         scale=rms[i0][:, h:h + 1],
                                         accum_out=psum_row[i0][:, h:h + 1]).then_inc(ev[f"exp{h}"], 1)

                for kt in range(1, KT):
                    if st.has(-1, STEPS):
                        probs_hi(kt)
                    if st.has(0, STEPS) and kt > 1:
                        exps(kt - 2)
                if st.has(1, STEPS):
                    act.wait_ge(ev["q_put"], st.past(1))
                    act.wait_ge(ev["s_put3"], st.past())
                    nc.scalar.copy(qt_hi[:, :], ring[1][:, :]).then_inc(ev["q_hi"], 1)
                if st.has(0, STEPS):
                    exps(G - 1)

            run_steps(act, FIRST, LOOP0, LOOP1, END, body)

        @block.gpsimd
        def _(pool):
            nc.gpsimd.memset(half_neg[:, :], -0.5).then_inc(s_half, 1)
            pool.wait_ge(s_half, 1)

            def body(st):
                i0, i1 = st.parity(), st.parity(1)
                if st.has(1, STEPS):
                    pool.wait_ge(ev["qkv_out"], st.past(1))
                    pool.wait_ge(s_rope[st.parity(1)], st.loads(1))
                    nc.gpsimd.tensor_tensor(q_cos[:, :].rearrange("p (h d) -> p h d", h=G),
                                            qkv[:, 0:G * D].rearrange("p (h d) -> p h d", h=G),
                                            rope[i1][:, 0:D].unsqueeze(1).to_broadcast([128, G, D]),
                                            ALU.mult).then_inc(ev["q_cos_out"], 1)
                    pool.wait_ge(ev["ss_out"], st.past(1))
                    pool.wait_ge(ev["exp3"], st.past(-1))
                    pool.wait_ge(ev["nb3"], st.past(-1))
                    st.hold()
                    nc.gpsimd.tensor_scalar(rms[i1][:, :], ssum[:, :], 1.0 / D, NORM_EPS, ALU.mult, ALU.add).then_inc(ev["ms"], 1)
                    pool.wait_ge(ev["ms"], st.past(1))
                    nc.gpsimd.tensor_tensor(rms[i1][:, :], rms[i1][:, :], half_neg[:, :], ALU.pow).then_inc(ev["rms_out"], 1)
                    pool.wait_ge(ev["q_sin_out"], st.past(1))
                    pool.wait_ge(ev["q_put"], st.past())
                    nc.gpsimd.tensor_tensor(q_rot[:, :], q_cos[:, :], q_sin[:, :], ALU.add).then_inc(ev["q_sum"], 1)
                if st.has(0, CHUNKS - AHEAD):
                    pool.wait_ge(ev["w_hi_out"], st.past())
                    at = st.number(lambda v: ((v + AHEAD) >> 3 & 1) * WCOLS + ((v + AHEAD) & (B - 1)) * WC)
                    nc.gpsimd.tensor_tensor(w_lo[:, bass.ds(at, WC)], raw[i0][:, :],
                                            w_hi[:, bass.ds(at, WC)].bitcast(F32), ALU.subtract).then_inc(ev["w_lo_out"], 1)
                elif st.fixed and 0 <= st.value < STEPS:
                    pool.sem_inc(ev["w_lo_out"], 1)
                if st.has(1, STEPS):
                    pool.wait_ge(s_kv[st.parity(1)], st.loads(1, NPP))
                    pool.wait_ge(ev["pv4"], st.past(-1))
                    st.hold()
                    nc.gpsimd.tensor_copy(v_hi[i1][:, 0:CT, :], kv[i1][:, :, D:2 * D])
                    nc.gpsimd.tensor_copy(v_hi[i1][:, CT, :], qkv[:, WP - D:WP]).then_inc(ev["v_hi_out"], 1)
                    pool.wait_ge(ev["v_hi_out"], st.past(1))
                    nc.gpsimd.tensor_tensor(v_lo[i1][:, 0:CT, :], kv[i1][:, :, D:2 * D],
                                            v_hi[i1][:, 0:CT, :].bitcast(F32), ALU.subtract)
                    nc.gpsimd.tensor_tensor(v_lo[i1][:, CT, :], qkv[:, WP - D:WP],
                                            v_hi[i1][:, CT, :].bitcast(F32), ALU.subtract).then_inc(ev["v_out"], 1)

            run_steps(pool, FIRST, LOOP0, LOOP1, END, body, s_spare)

        @block.vector
        def _(dve):

            def body(st):
                i0, i1 = st.parity(), st.parity(1)

                def probs_lo(kt):
                    u = st.parity(-1 + kt)
                    dve.wait_ge(ev[f"pt_hi_out{kt}"], st.past(-1))
                    nc.vector.tensor_tensor(pt_lo[u][:, :], ring[kt % 2][:, :], pt_hi[u][:, :].bitcast(F32),
                                            ALU.subtract).then_inc(ev[f"pt_lo_out{kt}"], 1)

                def output_lo():
                    dve.wait_ge(ev["o_hi_out"], st.past(-2))
                    nc.vector.tensor_tensor(o_lo[:, :], o_bank[:, :], o_hi[:, :].bitcast(F32), ALU.subtract).then_inc(ev["o_lo_out"], 1)

                ending = not st.has(1, STEPS)
                if st.has(-2, STEPS) and ending:
                    output_lo()
                if st.has(-1, STEPS):
                    dve.wait_ge(ev["exp3"], st.past(-1))
                    nc.vector.reciprocal(rsum[:, :], psum_row[i1][:, :]).then_inc(ev["rs"], 1)
                    dve.wait_ge(ev["rs"], st.past(-1))
                    for h in heads:
                        last = nc.vector.tensor_scalar(prob[i1][:, h, :], prob[i1][:, h, :], rsum[:, h:h + 1], None, ALU.mult)
                    last.then_inc(ev["norm"], 1)
                if st.has(0, STEPS):
                    dve.wait_ge(ev["kc_hi"], st.past())
                    nc.vector.tensor_tensor(kt_lo[:, 0:L], ring[0][:, :], kt_hi[:, 0:L].bitcast(F32), ALU.subtract).then_inc(ev["kc_lo"], 1)
                if st.has(-2, STEPS) and not ending:
                    output_lo()
                if st.has(0, STEPS):
                    dve.wait_ge(ev["kn_hi"], st.past())
                    nc.vector.tensor_tensor(kt_lo[:, L:KEYS], ring[1][:, 0:S], kt_hi[:, L:KEYS].bitcast(F32),
                                            ALU.subtract).then_inc(ev["kn_lo"], 1)
                if st.has(1, STEPS):
                    dve.wait_ge(s_rope[st.parity(1)], st.loads(1))
                    dve.wait_ge(ev["qkv_out"], st.past(1))
                    dve.wait_ge(ev["q_sum"], st.past())
                    qs = q_sin[:, :].rearrange("p (h d) -> p h d", h=G)
                    qp = qkv[:, 0:G * D].rearrange("p (h d) -> p h d", h=G)
                    half = D // 2
                    for lo, hi in ((0, half), (half, 0)):
                        last = nc.vector.tensor_tensor(qs[:, :, lo:lo + half], qp[:, :, hi:hi + half],
                                                       rope[i1][:, D + lo:D + lo + half].unsqueeze(1).to_broadcast([128, G, half]),
                                                       ALU.mult)
                    last.then_inc(ev["q_sin_out"], 1)
                    dve.wait_ge(ev["sq_out"], st.past(1))
                    nc.vector.reduce_sum(ssum[:, :], sq[:, :].rearrange("p (h d) -> p h d", h=G + 1), AX).then_inc(ev["ss_out"], 1)
                if st.has(-1, STEPS):
                    probs_lo(0)
                if st.has(-2, STEPS):
                    b = st.number(lambda v: ((v - 2) & (B - 1)) * DM)
                    dve.wait_ge(ev["wo_done"], st.past(-2))
                    at = attn[:, bass.ds(b, DM)]
                    nc.vector.tensor_tensor(at, wo_bank[:, :], at, ALU.add).then_inc(ev["acc"], 1)
                by_half = by_bank = lambda ap: ap.rearrange("p (b n) -> p b n", b=2)
                for h in heads:
                    if st.has(-1, STEPS):
                        probs_lo(h + 1)
                    if st.has(0, STEPS):
                        if h == 0:
                            dve.wait_ge(s_mask[st.parity()], st.loads())
                        dve.wait_ge(ev[f"exp{h - 2}" if h >= 2 else f"exp{h + 2}"], st.past(0 if h >= 2 else -1))
                        dve.wait_ge(ev[f"s_put{h}"], st.past())
                        st.hold()
                        nc.vector.tensor_tensor_reduce(out=by_half(score[h % 2][:, :]), in0=by_bank(slot[st.parity(1 + h)][:, :])[:, :, 0:HALF],
                                                       in1=by_half(mask[i0][:, :]), scale=1.0, scalar=LOWEST, op0=ALU.add,
                                                       op1=ALU.max, accum_out=top[:, h:h + 1]).then_inc(ev[f"mx{h}"], 1)
                        dve.wait_ge(ev[f"mx{h}"], st.past())
                        nc.vector.tensor_scalar(nbias[:, h:h + 1], top[:, h:h + 1], rms[i0][:, h:h + 1], -1.0,
                                                ALU.mult, ALU.mult).then_inc(ev[f"nb{h}"], 1)
                    if h == 0 and st.has(1, STEPS):
                        kc = qkv[:, G * D:(G + 1) * D]
                        rk = rms[i1][:, G:G + 1]
                        dve.wait_ge(ev["rms_out"], st.past(1))
                        nc.vector.scalar_tensor_tensor(out=k_cos[:, :], in0=kc, scalar=rk, in1=rope[i1][:, 2 * D:3 * D],
                                                       op0=ALU.mult, op1=ALU.mult)
                        for lo, hi in ((0, half), (half, 0)):
                            last = nc.vector.scalar_tensor_tensor(out=k_sin[:, lo:lo + half], in0=kc[:, hi:hi + half], scalar=rk,
                                                                  in1=rope[i1][:, 3 * D + lo:3 * D + lo + half],
                                                                  op0=ALU.mult, op1=ALU.mult)
                        last.then_inc(ev["k_parts"], 1)
                    if h == 1 and st.has(1, STEPS):
                        dve.wait_ge(ev["k_parts"], st.past(1))
                        dve.wait_ge(ev["kn_put"], st.past())
                        nc.vector.tensor_tensor(k_rot[:, :], k_cos[:, :], k_sin[:, :], ALU.add).then_inc(ev["k_sum"], 1)
                if st.has(1, STEPS):
                    dve.wait_ge(ev["q_hi"], st.past(1))
                    nc.vector.tensor_tensor(qt_lo[:, :], ring[1][:, :], qt_hi[:, :].bitcast(F32), ALU.subtract).then_inc(ev["q_lo"], 1)

            run_steps(dve, FIRST, LOOP0, LOOP1, END, body, s_spare)


def last_layer(nc, sem_ctx, s_spare, t, shared, scratch, out):
    _, x1b_dram, _, _ = scratch
    ident, attn = shared.ident, shared.attn
    had = shared.w_hi[:, 0:CH * DM]
    w8_hi, w8_lo = (w[:, CH * DM:2 * CH * DM] for w in (shared.w_hi, shared.w_lo))
    ctx = ExitStack()
    with ctx:
        def sb(name, shape, dt=F32):
            return ctx.enter_context(nc.sbuf_tensor(name, shape, dt))

        def sem(name):
            return sem_ctx.enter_context(nc.semaphore(name))

        two = range(2)
        a_st = [sb(f"a_st{p}", [128, DM]) for p in two]
        at_hi = [sb(f"at_hi{p}", [128, CH * S], F32R) for p in two]
        at_lo = [sb(f"at_lo{p}", [128, CH * S], F32R) for p in two]
        xh = [sb(f"xh{p}", [128, DM]) for p in two]
        amax, sx, rsx = ([sb(f"{n}{p}", [128, 1]) for p in two] for n in ("amax", "sx", "rsx"))
        sx_early = sb("sx_early", [128, 1])
        xabs = sb("xabs", [128, DM])
        v = [sb(f"v{p}", [128, DM]) for p in two]
        step = [sb(f"step{p}", [128, DM]) for p in two]
        qv = [sb(f"qv{p}", [128, DM]) for p in two]
        qt = [sb(f"qt{p}", [128, CH * S], F32R) for p in two]
        x1b = [sb(f"x1bf{p}", [128, DM]) for p in two]
        y = [sb(f"y{p}", [128, DM]) for p in two]
        res = [sb(f"res{p}", [128, DM]) for p in two]
        bank = {n: [ctx.enter_context(nc.psum_tensor(f"{n}{p}", [128, 512], F32)) for p in two]
                for n in ("a_bank", "h_bank", "q_bank", "f_bank")}

        ev = shared.ev
        s_x1b = [sem(f"s_x1b{p}") for p in two]
        s_out = [sem(f"s_out{p}") for p in two]
        block = ctx.enter_context(nc.Block())
        FIRST, END = -2, B + 2

        @block.sync
        def _(sp):
            def body(st):
                p = st.parity()
                if st.has(0, B):
                    sp.wait_ge(ev["res_out"], st.past(-2))
                    st.hold()
                    sp.dma_start(x1b[p][:, :], flat(x1b_dram[bass.ds(st.value, 1)])).then_inc(s_x1b[p], 16)
                if st.has(-2, B):
                    sp.wait_ge(ev["res_out"], st.past(-2))
                    st.hold()
                    sp.dma_start(flat(out[bass.ds(st.number(lambda i: i - 2), 1)]), res[p][:, :]).then_inc(s_out[p], 16)

            run_steps(sp, 0, 2, B, END, body, s_spare)
            for p in two:
                sp.wait_ge(s_out[p], 16 * B // 2)

        @block.tensor
        def _(pe):

            def transpose(dst, src):
                for c in range(CH):
                    last = nc.tensor.transpose(dst[:, c * 128:(c + 1) * 128], src[:, c * 128:(c + 1) * 128], ident[:, :])
                return last

            def body(st):
                p, q = st.parity(), st.parity(1)
                if st.has(1, B):
                    pe.wait_ge(ev["a_out"], st.past(1))
                    pe.wait_ge(ev["at_lo_out"], st.past(-1))
                    transpose(bank["a_bank"][q], a_st[q]).then_inc(ev["at_put"], 1)
                if st.has(-2, B):
                    pe.wait_ge(ev["q_out"], st.past(-2))
                    pe.wait_ge(ev["qt8_out"], st.past(-4))
                    transpose(bank["q_bank"][p], qv[p]).then_inc(ev["qt8_put"], 1)
                if st.has(0, B):
                    pe.wait_ge(ev["at_lo_out"], st.past())
                    pe.wait_ge(ev["xh_out"], st.past(-2))
                    for c in range(CH):
                        h = had[:, c * DM:(c + 1) * DM]
                        nc.tensor.matmul(bank["h_bank"][p][:, :], at_hi[p][:, c * S:(c + 1) * S], h, start=c == 0, stop=False)
                        last = nc.tensor.matmul(bank["h_bank"][p][:, :], at_lo[p][:, c * S:(c + 1) * S], h,
                                                start=False, stop=c == CH - 1)
                    last.then_inc(ev["rot"], 1)
                if st.has(-2, B):
                    pe.wait_ge(ev["qt8_out"], st.past(-2))
                    pe.wait_ge(ev["y_out"], st.past(-4))
                    for c in range(CH):
                        a = qt[p][:, c * S:(c + 1) * S]
                        nc.tensor.matmul(bank["f_bank"][p][:, :], a, w8_hi[:, c * DM:(c + 1) * DM], start=c == 0, stop=False)
                        last = nc.tensor.matmul(bank["f_bank"][p][:, :], a, w8_lo[:, c * DM:(c + 1) * DM],
                                                start=False, stop=c == CH - 1)
                    last.then_inc(ev["ffn"], 1)

            run_steps(pe, FIRST, 4, B - 2, END, body)

        @block.scalar
        def _(act):

            def body(st):
                p, q = st.parity(), st.parity(1)
                if st.has(-1, B):
                    act.wait_ge(ev["rsx_out"], st.past(-1))
                    act.wait_ge(ev["q_out"], st.past(-3))
                    nc.scalar.activation(v[q][:, :], xh[q][:, :], ACT.Copy, scale=rsx[q][:, :]).then_inc(ev["scaled"], 1)
                if st.has(1, B):
                    act.wait_ge(ev["at_put"], st.past(1))
                    act.wait_ge(ev["rot"], st.past(-1))
                    nc.scalar.copy(at_hi[q][:, :], bank["a_bank"][q][:, :]).then_inc(ev["at_hi_out"], 1)
                if st.has(-2, B):
                    act.wait_ge(ev["qt8_put"], st.past(-2))
                    act.wait_ge(ev["ffn"], st.past(-4))
                    nc.scalar.copy(qt[p][:, :], bank["q_bank"][p][:, :]).then_inc(ev["qt8_out"], 1)
                if st.has(2, B):
                    act.wait_ge(ev["at_put"], st.past())
                    at = bass.ds(st.number(lambda i: (i + 2) * DM), DM)
                    nc.scalar.copy(a_st[p][:, :], attn[:, at]).then_inc(ev["a_out"], 1)
                if st.has(0, B):
                    act.wait_ge(ev["xh_out"], st.past())
                    act.wait_ge(ev["amax_out"], st.past(-1))
                    nc.scalar.activation(xabs[:, :], xh[p][:, :], ACT.Abs).then_inc(ev["abs_out"], 1)

            run_steps(act, FIRST, 4, B - 2, END, body)

        @block.vector
        def _(dve):

            def body(st):
                p, q = st.parity(), st.parity(1)
                if st.has(-1, B):
                    dve.wait_ge(ev["scaled"], st.past(-1))
                    dve.wait_ge(ev["q_out"], st.past(-3))
                    nc.vector.tensor_scalar(step[q][:, :].bitcast(U32), v[q][:, :].bitcast(U32), EXP_BITS, None,
                                            ALU.bitwise_and).then_inc(ev["expo"], 1)
                    dve.wait_ge(ev["expo"], st.past(-1))
                    nc.vector.tensor_scalar(step[q][:, :], step[q][:, :], MIN_E4M3, ROUND_E4M3, ALU.max,
                                            ALU.mult).then_inc(ev["step_out"], 1)
                if st.has(1, B):
                    dve.wait_ge(ev["at_hi_out"], st.past(1))
                    nc.vector.tensor_tensor(at_lo[q][:, :], bank["a_bank"][q][:, :], at_hi[q][:, :].bitcast(F32),
                                            ALU.subtract).then_inc(ev["at_lo_out"], 1)
                if st.has(0, B):
                    dve.wait_ge(ev["rot"], st.past())
                    dve.wait_ge(ev["scaled"], st.past(-2))
                    nc.vector.tensor_scalar(xh[p][:, :], bank["h_bank"][p][:, :], DM ** -0.5, None, ALU.mult).then_inc(ev["xh_out"], 1)
                    dve.wait_ge(ev["abs_out"], st.past())
                    nc.vector.reduce_max(amax[p][:, :], xabs[:, :], AX).then_inc(ev["amax_out"], 1)
                    dve.wait_ge(ev["amax_out"], st.past())
                    nc.vector.tensor_scalar(sx_early[:, :], amax[p][:, :], 1.0 / FP8_MAX, None, ALU.mult).then_inc(ev["sx_early_out"], 1)
                    dve.wait_ge(ev["sx_early_out"], st.past())
                    dve.wait_ge(ev["scaled"], st.past(-2))
                    nc.vector.reciprocal(rsx[p][:, :], sx_early[:, :]).then_inc(ev["rsx_out"], 1)
                if st.has(-2, B):
                    dve.wait_ge(ev["ffn"], st.past(-2))
                    dve.wait_ge(ev["sx_out"], st.past(-2))
                    dve.wait_ge(ev["res_out"], st.past(-4))
                    nc.vector.scalar_tensor_tensor(out=y[p][:, :], in0=bank["f_bank"][p][:, :], scalar=sx[p][:, :],
                                                   in1=shared.scales[:, :], op0=ALU.mult, op1=ALU.mult).then_inc(ev["y_out"], 1)
                if st.has(0, B):
                    dve.wait_ge(ev["y_out"], st.past(-2))
                    nc.vector.tensor_scalar(sx[p][:, :], amax[p][:, :], 1.0 / FP8_MAX, None, ALU.mult).then_inc(ev["sx_out"], 1)

            run_steps(dve, FIRST, 4, B - 2, END, body)

        @block.gpsimd
        def _(pool):

            def body(st):
                p, q = st.parity(), st.parity(1)
                if st.has(-1, B):
                    pool.wait_ge(ev["step_out"], st.past(-1))
                    nc.gpsimd.tensor_tensor(v[q][:, :], v[q][:, :], step[q][:, :], ALU.add).then_inc(ev["q_add"], 1)
                    pool.wait_ge(ev["q_add"], st.past(-1))
                    pool.wait_ge(ev["qt8_put"], st.past(-3))
                    nc.gpsimd.tensor_tensor(qv[q][:, :], v[q][:, :], step[q][:, :], ALU.subtract).then_inc(ev["q_out"], 1)
                if st.has(-2, B):
                    pool.wait_ge(s_x1b[st.parity(-2)], st.loads(-2))
                    pool.wait_ge(ev["y_out"], st.past(-2))
                    if not st.fixed or st.value >= 4:
                        pool.wait_ge(s_out[st.parity(-4)], st.loads(-4))
                    nc.gpsimd.tensor_tensor(res[p][:, :], y[p][:, :], x1b[p][:, :], ALU.add).then_inc(ev["res_out"], 1)

            run_steps(pool, FIRST, 4, B - 2, END, body)


class Shared:

    def __init__(self, nc, ctx, sem_ctx):
        def sb(name, shape, dt=F32):
            return ctx.enter_context(nc.sbuf_tensor(name, shape, dt))

        def sems(name):
            return [sem_ctx.enter_context(nc.semaphore(f"{name}{p}")) for p in two]

        two = range(2)
        self.ident = sb("ident", [128, 128])
        self.attn = sb("attn", [128, B * DM])
        self.scales = sb("scales", [128, DM])
        self.pages = sb("pages", [1, B * NPP], I32)
        self.w_hi, self.w_lo = (sb(n, [128, 2 * WCOLS], F32R) for n in ("w_hi", "w_lo"))
        self.kv = [sb(f"kv{p}", [128, CT, 2 * D]) for p in two]
        self.x1t = [sb(f"x1ts{p}", [128, 2 * CH * S], F32R) for p in two]
        self.rope = [sb(f"rope{p}", [128, 4 * D]) for p in two]
        self.mask = [sb(f"mask{p}", [128, KEYS]) for p in two]
        self.x1b_odd = sb("x1b1", [128, DM])
        self.x1t_odd = sb("x1t1", [128, 2 * CH * S], F32R)
        self.s_st = sems("s_st")
        self.ev, self.by_engine = {}, {}
        for phase in (FIRST_EVENTS, ATTENTION_EVENTS, LAST_EVENTS):
            for engine, event_names in phase.items():
                for name in event_names.split():
                    self.ev[name] = sem_ctx.enter_context(nc.semaphore(name))
                    self.by_engine.setdefault(engine, []).append(self.ev[name])
        self.s_kv, self.s_x1t, self.s_rope, self.s_mask = (sems(n) for n in ("s_kv", "s_x1t", "s_rope", "s_mask"))


def build(nc, t, out):
    scratch = (
        nc.dram_tensor("x1t_scratch", (B, 128, 2 * CH * S), F32, kind="Internal").ap(),
        nc.dram_tensor("x1b_scratch", (B, S, DM), F32, kind="Internal").ap(),
        nc.dram_tensor("rope_scratch", (B, 128, 4 * D), F32, kind="Internal").ap(),
        nc.dram_tensor("mask_scratch", (B, 1, KEYS), F32, kind="Internal").ap(),
    )
    with ExitStack() as sem_ctx, ExitStack() as ctx:
        shared = Shared(nc, ctx, sem_ctx)
        s_spare = sem_ctx.enter_context(nc.semaphore("s_spare"))
        first_layer(nc, sem_ctx, s_spare, t, shared, scratch)
        attention(nc, sem_ctx, s_spare, t, shared, scratch)
        last_layer(nc, sem_ctx, s_spare, t, shared, scratch, out)


def hadamard(np, n):
    h = np.ones((1, 1), np.float32)
    while len(h) < n:
        h = np.block([[h, h], [h, -h]])
    return h


def chunked(np, w):
    n, k = w.shape
    return np.ascontiguousarray(w.reshape(n, k // 128, 128).transpose(2, 1, 0).reshape(128, -1))


def kernel(x, itok_B_1_14, itok_Bx16_0_63, itok_B_207_1644, L0_cond_weight, L0_ffn_W_base, L0_ffn_b_base,
           L0_ffn_lora_A, L0_ffn_lora_B, L0_ffn_router_W, L0_ffn_router_b, L0_ffn_domain_prior, L0_ffn_active,
           L1_cond_Wq, L1_cond_Wk, L1_cond_Wv, L1_cond_Wo, L1_cond_q_norm_w, L1_cond_k_norm_w, L1_cond_k_cache,
           L1_cond_v_cache, L1_ffn_weight_q, L1_ffn_scales, L1_ffn_bias):
    import numpy as np
    import concourse.bacc as bacc
    from concourse.bass_utils import run_bass_kernel_spmd

    a = {k: np.asarray(v) for k, v in dict(locals()).items() if hasattr(v, "shape") and hasattr(v, "dtype")}
    x = a["x"]
    base = np.concatenate([a["L0_ffn_W_base"], a["L0_ffn_lora_A"].reshape(ZCOLS, DM), a["L0_ffn_router_W"]])
    adapter_w = a["L0_cond_weight"].reshape(ADAPTERS, DM, CH, 128).transpose(0, 3, 2, 1)
    wq = a["L1_cond_Wq"].reshape(HK, G * D, CH, 128).transpose(0, 3, 2, 1)
    wk = a["L1_cond_Wk"].reshape(HK, D, CH, 128).transpose(0, 3, 2, 1)
    wv = a["L1_cond_Wv"].reshape(HK, D, CH, 128).transpose(0, 3, 2, 1)
    wo = a["L1_cond_Wo"].reshape(DM, HK, G, D).transpose(1, 3, 2, 0)
    weights = np.concatenate([np.concatenate([wq, wk, wv], 3).reshape(HK, 128, CH * WP), wo.reshape(HK, 128, G * DM)], 2)
    last = np.concatenate([chunked(np, hadamard(np, DM)), chunked(np, a["L1_ffn_weight_q"]),
                           np.zeros((128, WCOLS - 2 * CH * DM), np.float32)], 1)
    weights = np.concatenate([weights, last[None]])
    weights = weights.reshape(HK + 1, 128, B, WC).transpose(0, 2, 1, 3).reshape(CHUNKS, 128, WC)
    kv = np.concatenate([a["L1_cond_k_cache"], a["L1_cond_v_cache"]], 3).transpose(2, 0, 1, 3)
    inv_freq = np.float32(1.0) / np.float32(10000.0) ** (np.arange(0, D, 2, dtype=np.float32) / np.float32(D))
    row = lambda v: v.reshape(1, -1)
    arrays = {
        "x": x,
        "xt": x.reshape(B, S, CH, 128).transpose(0, 3, 2, 1).reshape(B, 128, CH * S),
        "adapter_w": adapter_w.reshape(ADAPTERS, 128, CH * DM),
        "adapters": row(a["itok_B_1_14"]),
        "w0": base.reshape(L0COLS, CH, 128).transpose(2, 1, 0),
        "lora_b": a["L0_ffn_lora_B"].transpose(0, 2, 1).reshape(ZCOLS, DM),
        "biases": row(np.concatenate([a["L0_ffn_b_base"], a["L1_ffn_bias"]])),
        "small_rows": row(np.concatenate([a["L0_ffn_router_b"], a["L0_ffn_domain_prior"], inv_freq,
                                          a["L1_cond_q_norm_w"], a["L1_cond_k_norm_w"]])),
        "ints": row(np.concatenate([a["L0_ffn_active"], a["itok_B_207_1644"]])),
        "block_table": row(a["itok_Bx16_0_63"].reshape(-1)),
        "weights": weights,
        "kv": kv,
        "scales": row(a["L1_ffn_scales"]),
    }
    arrays = {k: np.ascontiguousarray(v) for k, v in arrays.items()}

    nc = bacc.Bacc("TRN2", target_bir_lowering=False, num_devices=1)
    t = {k: nc.dram_tensor(f"in_{k}", v.shape, mybir.dt.from_np(v.dtype), kind="ExternalInput").ap()
         for k, v in arrays.items()}
    out = nc.dram_tensor("out", (B, S, DM), F32, kind="ExternalOutput").ap()
    build(nc, t, out)
    r = run_bass_kernel_spmd(nc, [{f"in_{k}": v for k, v in arrays.items()}], core_ids=[0])
    return r.results[0]["out"]
```
